# Optimizing a Trainium2 kernel written in Bass

```python
import numpy as np
import jax
import jax.numpy as jnp

def _softmax(x, axis=-1):
    return jax.nn.softmax(x, axis=axis)

def _gelu(x):
    return jax.nn.gelu(x, approximate=True)

def _silu(x):
    return jax.nn.silu(x)

def _sigmoid(x):
    return jax.nn.sigmoid(x)

def _layernorm(x, axis=-1, eps=1e-05):
    m = jnp.mean(x, axis=axis, keepdims=True)
    v = jnp.var(x, axis=axis, keepdims=True)
    return (x - m) / jnp.sqrt(v + eps)

def _scatter_add(tgt, idx, src, axis=0):
    return tgt.at[idx].add(src)

def _segment_sum(src, seg, n):
    return jax.ops.segment_sum(src, seg, n)
kernel_name = 'mk_flamingo_gated_d1_seqx_r8_e623b3'

def setup_inputs(seed: int=0):
    np.random.seed(seed)
    _w = jnp.asarray

    def _rec_inputs():
        import jax
        import jax.numpy as jnp
        _rk = jax.random.key(seed)
        x = 7.22e-05 + 1 * jax.random.normal(jax.random.fold_in(_rk, 1), (64, 128, 128), jnp.float32)
        _lenS = 128 - jax.random.randint(jax.random.fold_in(_rk, 7), (64,), 0, max(1, 128 // 4) + 1, jnp.int32)
        _lenS2 = 120 - jax.random.randint(jax.random.fold_in(_rk, 8), (64,), 0, max(1, 120 // 4) + 1, jnp.int32)
        _ctx_1024P = jax.random.normal(jax.random.fold_in(_rk, 11), (64, 16, 128), jnp.float32)
        _ctx_1024c = jax.random.dirichlet(jax.random.fold_in(_rk, 511), 0.3 * jnp.ones((16,), jnp.float32), (64, 120))
        _ctx_1024t = jnp.einsum('bsk,bkd->bsd', _ctx_1024c, _ctx_1024P)
        _ctx_1024t = _ctx_1024t * jax.lax.rsqrt(jnp.mean(jnp.square(_ctx_1024t)) + 1e-12) * 0.953939
        ctx_1024 = 4.13588e-05 + 0.999923 * (_ctx_1024t + 0.3 * jax.random.normal(jax.random.fold_in(_rk, 611), (64, 120, 128), jnp.float32))
        _g = jax.random.normal(jax.random.fold_in(_rk, 9001), (2, 1), jnp.float32)
        _g = jnp.sign(_g) * jnp.maximum(jnp.abs(_g), 1.0) + (_g == 0) * 1.0
        g_xattn = _g[0]
        g_ffn = _g[1]
        return (x, ctx_1024, g_xattn, g_ffn)
    x, ctx_1024, g_xattn, g_ffn = _rec_inputs()

    def _L0_xattn_setup():
        import jax, jax.numpy as jnp
        import numpy as np
        import math
        B, S, H = (4, 256, 128)
        key = jax.random.key(seed)
        k1, k2, k3, k4 = jax.random.split(key, 4)
        queries = jax.random.normal(k1, (B, S, H), dtype=jnp.float32)
        keys = jax.random.normal(k2, (B, S, H), dtype=jnp.float32)
        values = jax.random.normal(k3, (B, S, H), dtype=jnp.float32)
        W_out = jax.random.normal(k4, (H, H), dtype=jnp.float32) * (1.0 / math.sqrt(H))
        b_out = jnp.zeros((H,), dtype=jnp.float32)
        return {'queries': queries, 'keys': keys, 'values': values, 'W_out': W_out, 'b_out': b_out}
    _L0_xattn_all = _L0_xattn_setup()
    _L0_xattn_in = {k: v for k, v in _L0_xattn_all.items() if k in ('W_out', 'b_out')}
    del _L0_xattn_all

    def _L0_ffn_setup():
        import jax, jax.numpy as jnp
        import numpy as np
        H = 128
        I = 256
        E = 8
        B, S = (2, 512)
        EPS = 1e-05
        INIT = 0.02

        def _layernorm(x, w, b):
            mu = jnp.mean(x, axis=-1, keepdims=True)
            var = jnp.mean(jnp.square(x - mu), axis=-1, keepdims=True)
            return (x - mu) * jax.lax.rsqrt(var + EPS) * w + b
        key = jax.random.key(seed)
        ks = jax.random.split(key, 9)
        return {'hidden_states': jax.random.normal(ks[0], (B, S, H), jnp.float32), 'ln_w': jnp.ones((H,), jnp.float32), 'ln_b': jnp.zeros((H,), jnp.float32), 'router_w': jax.random.normal(ks[1], (H, E), jnp.float32) * INIT, 'gate_w': jax.random.normal(ks[2], (E, H, I), jnp.float32) * INIT, 'up_w': jax.random.normal(ks[3], (E, H, I), jnp.float32) * INIT, 'down_w': jax.random.normal(ks[4], (E, I, H), jnp.float32) * INIT, 'sh_gate': jax.random.normal(ks[5], (H, I), jnp.float32) * INIT, 'sh_up': jax.random.normal(ks[6], (H, I), jnp.float32) * INIT, 'sh_down': jax.random.normal(ks[7], (I, H), jnp.float32) * INIT}
    _L0_ffn_all = _L0_ffn_setup()
    _L0_ffn_in = {k: v for k, v in _L0_ffn_all.items() if k in ('ln_w', 'ln_b', 'router_w', 'gate_w', 'up_w', 'down_w', 'sh_gate', 'sh_up', 'sh_down')}
    del _L0_ffn_all
    return {'x': x, 'ctx_1024': ctx_1024, 'g_xattn': g_xattn, 'g_ffn': g_ffn, 'L0_xattn_W_out': _L0_xattn_in['W_out'], 'L0_xattn_b_out': _L0_xattn_in['b_out'], 'L0_ffn_ln_w': _L0_ffn_in['ln_w'], 'L0_ffn_ln_b': _L0_ffn_in['ln_b'], 'L0_ffn_router_w': _L0_ffn_in['router_w'], 'L0_ffn_gate_w': _L0_ffn_in['gate_w'], 'L0_ffn_up_w': _L0_ffn_in['up_w'], 'L0_ffn_down_w': _L0_ffn_in['down_w'], 'L0_ffn_sh_gate': _L0_ffn_in['sh_gate'], 'L0_ffn_sh_up': _L0_ffn_in['sh_up'], 'L0_ffn_sh_down': _L0_ffn_in['sh_down']}

def reference(x, ctx_1024, g_xattn, g_ffn, L0_xattn_W_out, L0_xattn_b_out, L0_ffn_ln_w, L0_ffn_ln_b, L0_ffn_router_w, L0_ffn_gate_w, L0_ffn_up_w, L0_ffn_down_w, L0_ffn_sh_gate, L0_ffn_sh_up, L0_ffn_sh_down):
    import jax
    import jax.numpy as jnp

    def _L0_xattn_ref(queries, keys, values, W_out, b_out):
        import jax, jax.numpy as jnp
        import numpy as np
        import math
        B, S, H = (4, 256, 128)
        scale = 1.0 / math.sqrt(queries.shape[-1])
        scores = jnp.einsum('bqh,bkh->bqk', queries, keys) * scale
        distr = jax.nn.softmax(scores, axis=-1)
        out = jnp.einsum('bqk,bkh->bqh', distr, values)
        out = jnp.einsum('bqh,oh->bqo', out, W_out) + b_out
        return out

    def _L0_ffn_ref(hidden_states, ln_w, ln_b, router_w, gate_w, up_w, down_w, sh_gate, sh_up, sh_down):
        import jax, jax.numpy as jnp
        import numpy as np
        H = 128
        I = 256
        E = 8
        B, S = (2, 512)
        EPS = 1e-05
        INIT = 0.02

        def _layernorm(x, w, b):
            mu = jnp.mean(x, axis=-1, keepdims=True)
            var = jnp.mean(jnp.square(x - mu), axis=-1, keepdims=True)
            return (x - mu) * jax.lax.rsqrt(var + EPS) * w + b
        b, s, h = hidden_states.shape
        normed = _layernorm(hidden_states, ln_w, ln_b)
        xf = normed.reshape(-1, h)
        logits = xf @ router_w
        top_idx = jnp.argmax(logits, axis=-1)
        top_score = jax.nn.sigmoid(jnp.max(logits, axis=-1))

        def body(acc, ew):
            g, u, d, e = ew
            w = jnp.where(top_idx == e, top_score, 0.0)[:, None]
            xe = xf * w
            hmid = jax.nn.silu(xe @ g) * (xe @ u)
            return (acc + hmid @ d, None)
        routed, _ = jax.lax.scan(body, jnp.zeros_like(xf), (gate_w, up_w, down_w, jnp.arange(E)))
        shared = jax.nn.silu(xf @ sh_gate) * (xf @ sh_up) @ sh_down
        moe_out = (routed + shared).reshape(b, s, h)
        return hidden_states + moe_out
    x = x + jnp.tanh(g_xattn[0]) * _L0_xattn_ref(_layernorm(x, axis=-1), ctx_1024, ctx_1024, L0_xattn_W_out, L0_xattn_b_out)
    x = x + jnp.tanh(g_ffn[0]) * _L0_ffn_ref(_layernorm(x, axis=-1), L0_ffn_ln_w, L0_ffn_ln_b, L0_ffn_router_w, L0_ffn_gate_w, L0_ffn_up_w, L0_ffn_down_w, L0_ffn_sh_gate, L0_ffn_sh_up, L0_ffn_sh_down)
    return x

_drawn_inputs = setup_inputs


def setup_inputs(seed=0):
    import zlib

    import numpy as np

    out = dict(_drawn_inputs(seed))
    spreads = {'L0_xattn_b_out': (0.0, 0.1), 'L0_ffn_ln_w': (1.0, 0.6), 'L0_ffn_ln_b': (0.0, 0.8)}
    factors = {'L0_ffn_router_w': 3.861,
     'L0_ffn_gate_w': 3.584,
     'L0_ffn_up_w': 3.59,
     'L0_ffn_down_w': 3.602}
    for name, (base, spread) in spreads.items():
        noise = np.random.default_rng([zlib.crc32(name.encode()), seed]).standard_normal(out[name].shape)
        drawn = base * np.exp(spread * noise) if base else spread * noise
        out[name] = jnp.asarray(drawn.astype(out[name].dtype))
    for name, factor in factors.items():
        out[name] = (out[name] * factor).astype(out[name].dtype)
    return out
```

```python
from contextlib import ExitStack

import concourse.bass as bass
from concourse import mybir

ALU = mybir.AluOpType
ACT = mybir.ActivationFunctionType
F32 = mybir.dt.float32
BF16 = mybir.dt.bfloat16
I32 = mybir.dt.int32
AX_X = mybir.AxisListType.X

P = 128
EPS = 1e-5
GROUP = 4
RING = 4


def flamingo_kernel(nc, x, ctx_in, g_xattn, g_ffn, w_out, b_out, ln_w, ln_b, router_w,
                    gate_w, up_w, down_w, sh_gate, sh_up, sh_down, out):
    B, S, H = x.shape
    K = ctx_in.shape[1]
    E, _, I = gate_w.shape
    assert S == P and H == P and B % (GROUP * RING) == 0 and I == 2 * P
    GROUPS = B // GROUP
    PAIRS = GROUPS // 2
    PT = 2 * GROUP
    TOKENS = B * S
    CHUNKS = I // P
    REGION = TOKENS + P
    TILES = TOKENS // P + E
    assert TILES % RING == 0
    Z_SCALE, MEAN, VAR, SCORE, TOKEN = H, H + 1, H + 2, H + 3, H + 4
    ROW = H + 5
    NO_TOKEN = 1 << 20
    CONSTS = 10

    scratch = nc.dram_tensor("sorted_rows", [E * REGION + P, ROW], F32).ap()
    out_rows = out.rearrange("b s h -> (b s) h")
    x_v = x.rearrange("b s h -> s b h")
    ctx_v = ctx_in.rearrange("b k h -> k b h")

    with ExitStack() as stack:
        def sb(name, shape, dt=F32):
            return stack.enter_context(nc.sbuf_tensor(name, shape, dt))

        def sem(name):
            return stack.enter_context(nc.semaphore(name))

        banks = [stack.enter_context(nc.psum_tensor(f"bank{i}", [P, 512], F32)) for i in range(8)]

        ident = sb("ident", [P, P])
        ones = sb("ones", [P, P], BF16)
        before = sb("before", [P, P], BF16)
        expert_rev = sb("expert_rev", [P, E])
        half_powers = sb("half_powers", [P, 3, GROUP])
        gates = sb("gates", [P, 2])
        tanh_g = sb("tanh_g", [P, 2])
        w_out_sb = sb("w_out_sb", [P, H])
        w_out_t = sb("w_out_t", [P, H])
        bias_raw = sb("bias_raw", [P, H])
        bias_b = sb("bias_b", [P, H])
        lnw = sb("lnw", [P, 1])
        lnb = sb("lnb", [P, 1])
        router = sb("router", [P, E])
        gate_up = sb("gate_up", [P, E, 2 * I])
        down_raw = sb("down_raw", [P, E + 1, CHUNKS, H])
        down = sb("down", [P, E + 1, CHUNKS, H])
        sh_gu = sb("sh_gu", [P, 2 * I])

        x_sb = sb("x_sb", [P, RING, GROUP, H])
        ctx_sb = sb("ctx_sb", [P, RING, GROUP, H])
        x_st = sb("x_st", [P, GROUP, 6])
        x_mv = sb("x_mv", [P, GROUP, 2])
        x_ve = sb("x_ve", [P, GROUP])
        x_rs = sb("x_rs", [P, 2, GROUP])
        n1 = sb("n1", [P, 2, GROUP, H])
        n1T = sb("n1T", [P, GROUP * P])
        ctxT = sb("ctxT", [P, GROUP * K])
        neg_max = sb("neg_max", [P, 2, GROUP])
        probs = sb("probs", [P, GROUP, K])
        row_sum = sb("row_sum", [P, 2, GROUP])
        row_inv = sb("row_inv", [P, GROUP])
        probsT = sb("probsT", [P, GROUP * P])
        vals = sb("vals", [P, 2, GROUP * H])
        x1 = sb("x1", [P, GROUP, H])
        z_st = sb("z_st", [P, GROUP, 6])
        z_pw_in = sb("z_pw_in", [P, 3, GROUP])
        z_pw = sb("z_pw", [P, 2, 3, GROUP])
        z_t = sb("z_t", [P, GROUP])
        rows = sb("rows", [P, RING * GROUP, ROW])
        rows_i = rows[:, :, :].bitcast(I32)
        xfT = sb("xfT", [P, GROUP * P])
        lg = sb("lg", [P, PT, E])
        lg_max = sb("lg_max", [P, PT])
        hit = sb("hit", [P, PT, E])
        hit_rev = sb("hit_rev", [P, PT, E])
        best_rev = sb("best_rev", [P, PT])
        onehot = sb("onehot", [P, PT + 1, E], BF16)
        place = sb("place", [P, PT, E])
        place_hit = sb("place_hit", [P, PT, E])
        pos_f = sb("pos_f", [P, PT])
        pos = sb("pos", [P, 2, PT], I32)
        first_free = sb("first_free", [P, E])
        exp_lg = sb("exp_lg", [P, PT])
        exp_lg1 = sb("exp_lg1", [P, PT])

        region_at = sb("region_at", [P, E])
        counts = sb("counts", [P, E])
        steps128 = sb("steps128", [P, TOKENS // P])
        over = sb("over", [P, E, TOKENS // P])
        n_tiles = sb("n_tiles", [P, E])
        cum = sb("cum", [P, 4, E])
        tile_no = sb("tile_no", [P, TILES])
        past = sb("past", [P, TILES, E])
        past_cum = sb("past_cum", [P, TILES, E])
        tile_e = sb("tile_e", [P, TILES])
        tile_c = sb("tile_c", [P, TILES])
        tile_a = sb("tile_a", [P, TILES])
        tile_b = sb("tile_b", [P, TILES])
        tile_row = sb("tile_row", [P, TILES], I32)
        tile_expert = sb("tile_expert", [P, TILES], I32)
        fill_row = sb("fill_row", [P, E], I32)
        filling = sb("filling", [P, ROW])
        filling_i = filling[:, :].bitcast(I32)

        srow = sb("srow", [P, RING, ROW])
        srow_i = srow[:, :, :].bitcast(I32)
        token = sb("token", [P, RING], I32)
        base = sb("base", [P, RING, H])
        xfT2 = sb("xfT2", [P, 2, P])
        act_r = sb("act_r", [P, 2, I])
        act_s = sb("act_s", [P, 2, I])
        hid_r = sb("hid_r", [P, 2, I])
        hid_s = sb("hid_s", [P, 2, I])
        hidT_r = sb("hidT_r", [P, 2, I])
        res = sb("res", [P, RING, H])

        s_const = sem("s_const")
        s_const0 = sem("s_const0")
        s_small = sem("s_small")
        s_big = sem("s_big")
        s_tanh = sem("s_tanh")
        s_woT = sem("s_woT")
        s_wo = sem("s_wo")
        s_down = sem("s_down")
        x_in = [sem(f"x_in{i}") for i in range(RING)]
        c_in = [sem(f"c_in{i}") for i in range(RING)]
        s_xst, s_xmv, s_xve, s_xrs = sem("s_xst"), sem("s_xmv"), sem("s_xve"), sem("s_xrs")
        s_n1 = sem("s_n1")
        s_n1T_ps, s_ctxT_ps, s_n1T, s_ctxT = sem("s_n1T_ps"), sem("s_ctxT_ps"), sem("s_n1T"), sem("s_ctxT")
        s_sc, s_val_ps, s_val = sem("s_sc"), sem("s_val_ps"), sem("s_val")
        s_max, s_prob = sem("s_max"), sem("s_prob")
        s_pT_ps, s_pT, s_att = sem("s_pT_ps"), sem("s_pT"), sem("s_att")
        s_inv, s_x1, s_zst, s_zmv = sem("s_inv"), sem("s_x1"), sem("s_zst"), sem("s_zmv")
        s_zin, s_zpw, s_zt, s_zsc = sem("s_zin"), sem("s_zpw"), sem("s_zt"), sem("s_zsc")
        s_z, s_zT_ps, s_xfT, s_lg = sem("s_z"), sem("s_zT_ps"), sem("s_xfT"), sem("s_lg")
        s_lg_sb, s_lmax, s_hit, s_rev, s_best = sem("s_lg_sb"), sem("s_lmax"), sem("s_hit"), sem("s_rev"), sem("s_best")
        s_hot, s_rank, s_place, s_phit = sem("s_hot"), sem("s_rank"), sem("s_place"), sem("s_phit")
        s_free, s_posf, s_pos = sem("s_free"), sem("s_posf"), sem("s_pos")
        s_elg, s_elg1, s_score, s_token = sem("s_elg"), sem("s_elg1"), sem("s_score"), sem("s_token")
        sent = [sem(f"sent{i}") for i in range(RING)]
        s_tab = sem("s_tab")
        s_table = sem("s_table")
        s_fill = sem("s_fill")
        r_in = [sem(f"r_in{i}") for i in range(RING)]
        s_tok2, s_base = sem("s_tok2"), sem("s_base")
        s_zT2_ps, s_xfT2 = sem("s_zT2_ps"), sem("s_xfT2")
        s_gur, s_gus, s_ar, s_as = sem("s_gur"), sem("s_gus"), sem("s_ar"), sem("s_as")
        s_hr, s_hs, s_hT_ps, s_hT = sem("s_hr"), sem("s_hs"), sem("s_hT_ps"), sem("s_hT")
        s_dn, s_res = sem("s_dn"), sem("s_res")
        stored = [sem(f"stored{i}") for i in range(RING)]

        b_n1T, b_ctxT, b_sc, b_val, b_pT, b_att, b_zT, b_lg = banks
        lg_ps = b_lg[:, 0:PT * E].rearrange("p (t e) -> p t e", e=E)
        rank_ps = b_lg[:, 128:128 + (PT + 1) * E].rearrange("p (t e) -> p t e", e=E)
        b_zT2, b_hT = banks[0], banks[1]
        b_gur, b_gus, b_dn = banks[2:4], banks[4:6], banks[6:8]

        def after(u, c, least):
            return not isinstance(u, int) or RING * u + c >= least

        def run_steps(eng, step, last, first_looped, end_looped):
            for t in range(first_looped):
                step(0, t)
            with eng.Fori(first_looped // RING, end_looped // RING) as u:
                for c in range(RING):
                    step(u, c)
            for t in range(end_looped, last + 1):
                step(0, t)

        def live(u, c, count):
            return not isinstance(u, int) or 0 <= RING * u + c < count

        block = stack.enter_context(nc.Block())

        @block.sync
        def _(sp):
            def load_group(u, c):
                g, slot = RING * u + c, c % RING
                if after(u, c, RING):
                    sp.wait_ge(s_x1, g - RING + 1)
                sp.dma_start(x_sb[:, slot], x_v[:, bass.ds(g * GROUP, GROUP), :]).then_inc(x_in[slot], 16)
                if after(u, c, RING):
                    sp.wait_ge(s_ctxT_ps, g - RING + 1)
                sp.dma_start(ctx_sb[0:K, slot], ctx_v[:, bass.ds(g * GROUP, GROUP), :]).then_inc(c_in[slot], 16)

            load_group(0, 0)
            sp.dma_start(w_out_sb[:, :], w_out).then_inc(s_small, 16)
            sp.dma_start(bias_raw[:, :], b_out.rearrange("(a h) -> a h", a=1).to_broadcast([P, H])).then_inc(s_small, 16)
            sp.dma_start(gates[:, 0:1], g_xattn.rearrange("(a h) -> a h", a=1).to_broadcast([P, 1])).then_inc(s_small, 16)
            sp.dma_start(gates[:, 1:2], g_ffn.rearrange("(a h) -> a h", a=1).to_broadcast([P, 1])).then_inc(s_small, 16)
            sp.dma_start(lnw[:, :], ln_w.rearrange("(h a) -> h a", a=1)).then_inc(s_small, 16)
            sp.dma_start(lnb[:, :], ln_b.rearrange("(h a) -> h a", a=1)).then_inc(s_small, 16)
            sp.dma_start(router[:, :], router_w).then_inc(s_small, 16)
            for c in range(1, RING):
                load_group(0, c)
            sp.dma_start(down_raw[:, 0:E], down_w.rearrange("e (c p) h -> p e c h", p=P)).then_inc(s_big, 16)
            sp.dma_start(down_raw[:, E], sh_down.rearrange("(c p) h -> p c h", p=P)).then_inc(s_big, 16)
            sp.dma_start(gate_up[:, :, 0:I], gate_w.rearrange("e h i -> h e i")).then_inc(s_big, 16)
            sp.dma_start(gate_up[:, :, I:2 * I], up_w.rearrange("e h i -> h e i")).then_inc(s_big, 16)
            sp.dma_start(sh_gu[:, 0:I], sh_gate).then_inc(s_big, 16)
            sp.dma_start(sh_gu[:, I:2 * I], sh_up).then_inc(s_big, 16)
            with sp.Fori(1, GROUPS // RING) as u:
                for c in range(RING):
                    load_group(u, c)

            sp.wait_ge(s_table, 1)
            for e in range(E):
                at = sp.value_load(fill_row[0:1, e:e + 1], min_val=0, max_val=E * REGION)
                sp.dma_start(scratch[bass.ds(at, P), :], filling[:, :]).then_inc(s_fill, 16)
            sp.dma_start(scratch[E * REGION:E * REGION + P, :], filling[:, :]).then_inc(s_fill, 16)
            sp.wait_ge(s_fill, 16 * (E + 1))
            for slot in range(RING):
                sp.wait_ge(sent[slot], 16 * GROUP * (GROUPS // RING))

            def load_tile(u, c):
                k, slot = RING * u + c, c % RING
                if after(u, c, RING):
                    sp.wait_ge(s_base, k - RING + 1)
                    sp.wait_ge(s_zT2_ps, k - RING + 1)
                    sp.wait_ge(s_hr, k - RING + 1)
                at = sp.value_load(tile_row[0:1, bass.ds(k, 1)], min_val=0, max_val=E * REGION)
                sp.dma_start(srow[:, slot], scratch[bass.ds(at, P), :]).then_inc(r_in[slot], 16)

            for c in range(RING):
                load_tile(0, c)
            with sp.Fori(1, TILES // RING) as u:
                for c in range(RING):
                    load_tile(u, c)

        @block.gpsimd
        def _(pool):
            pool.memset(ident[:, :], 0.0).then_inc(s_const0, 1)
            pool.memset(before[:, :], 1.0).then_inc(s_const0, 1)
            pool.memset(ones[:, :], 1.0).then_inc(s_const, 1)
            pool.memset(half_powers[:, :, :], -0.5).then_inc(s_const0, 1)
            pool.memset(onehot[:, :, :], 0.0).then_inc(s_const, 1)
            pool.memset(filling[:, :], 0.0).then_inc(s_const0, 1)
            pool.wait_ge(s_const0, 4)
            pool.affine_select(out=ident[:, :], in_=ident[:, :], compare_op=ALU.not_equal, fill=1.0,
                               base=0, pattern=[[-1, P]], channel_multiplier=1).then_inc(s_const, 1)
            pool.affine_select(out=before[:, :], in_=before[:, :], compare_op=ALU.is_gt, fill=0.0,
                               base=0, pattern=[[1, P]], channel_multiplier=-1).then_inc(s_const, 1)
            pool.memset(half_powers[:, 1, :], 0.5).then_inc(s_const, 1)
            pool.memset(filling_i[:, TOKEN:TOKEN + 1], NO_TOKEN).then_inc(s_const, 1)
            pool.iota(expert_rev[:, :], pattern=[[-1, E]], base=E, channel_multiplier=0,
                      allow_small_or_imprecise_dtypes=True).then_inc(s_const, 1)
            pool.iota(first_free[:, :], pattern=[[REGION, E]], base=0, channel_multiplier=0,
                      allow_small_or_imprecise_dtypes=True).then_inc(s_free, 1)
            pool.iota(region_at[:, :], pattern=[[REGION, E]], base=0, channel_multiplier=0,
                      allow_small_or_imprecise_dtypes=True).then_inc(s_const, 1)
            pool.iota(steps128[:, :], pattern=[[P, TOKENS // P]], base=0, channel_multiplier=0,
                      allow_small_or_imprecise_dtypes=True).then_inc(s_const, 1)
            pool.iota(tile_no[:, :], pattern=[[1, TILES]], base=0, channel_multiplier=0,
                      allow_small_or_imprecise_dtypes=True).then_inc(s_const, 1)
            pool.iota(rows_i[:, :, TOKEN:TOKEN + 1], pattern=[[P, RING * GROUP], [0, 1]], base=0,
                      channel_multiplier=1).then_inc(s_token, RING)
            pool.wait_ge(s_const, CONSTS)
            spare_reg = pool.alloc_register("spare_pool")
            pool.reg_mov(spare_reg, 0)

            def wait_reg(sem, count):
                if not isinstance(count, int):
                    count = pool.to_reg(count)
                    pool.wait_ge(s_const, CONSTS)
                pool.wait_ge(sem, count)

            def x_scale(u, c):
                g = RING * u + c
                wait_reg(s_xmv, g + 1)
                pool.tensor_scalar(x_ve[:, :], x_mv[:, :, 1], EPS, float(H), ALU.add, ALU.mult).then_inc(s_xve, 1)
                wait_reg(s_xve, g + 1)
                pool.tensor_tensor(x_rs[:, c % 2, :], x_ve[:, :], half_powers[:, 0, :], ALU.pow).then_inc(s_xrs, 1)

            def z_scale(u, c):
                g, slot = RING * u + c, c % RING
                wait_reg(s_zmv, g + 1)
                var = rows[:, GROUP * slot:GROUP * slot + GROUP, VAR]
                pool.tensor_scalar(z_pw_in[:, 0, :], var, 1.0 + EPS, EPS * EPS, ALU.mult, ALU.add).then_inc(s_zin, 1)
                pool.tensor_scalar(z_pw_in[:, 1, :], var, 1.0 + EPS, EPS * EPS, ALU.mult, ALU.add).then_inc(s_zin, 1)
                pool.tensor_scalar(z_pw_in[:, 2, :], var, EPS, None, ALU.add).then_inc(s_zin, 1)
                wait_reg(s_zin, 3 * (g + 1))
                pool.tensor_tensor(z_pw[:, c % 2], z_pw_in[:, :, :], half_powers[:, :, :], ALU.pow).then_inc(s_zpw, 1)

            def z_back(u, c):
                g, slot = RING * u + c, c % RING
                wait_reg(s_zpw, g + 1)
                pool.tensor_scalar(z_t[:, :], z_pw[:, c % 2, 2, :], tanh_g[:, 1:2], 1.0, ALU.mult, ALU.add).then_inc(s_zt, 1)
                wait_reg(s_zt, g + 1)
                pool.tensor_tensor(rows[:, GROUP * slot:GROUP * slot + GROUP, Z_SCALE], z_t[:, :],
                                   z_pw[:, c % 2, 1, :], ALU.mult).then_inc(s_zsc, 1)

            def scatter(u, c):
                g, slot = RING * u + c, c % RING
                p = 2 * u + c // 2
                wait_reg(s_pos, p + 1)
                wait_reg(s_score, p + 1)
                wait_reg(s_zsc, g + 1)
                wait_reg(s_token, g + 1)
                for j in range(GROUP):
                    pool.indirect_dma_start(
                        out=scratch, out_offset=bass.IndirectOffsetOnAxis(
                            ap=pos[:, (c // 2) % 2, (c % 2) * GROUP + j:(c % 2) * GROUP + j + 1], axis=0),
                        in_=rows[:, GROUP * slot + j, :], in_offset=None).then_inc(sent[slot], 16)

            def next_tokens(u, c):
                g, slot = RING * u + c, c % RING
                wait_reg(sent[slot], 16 * GROUP * (u + c // RING + 1))
                mine = rows_i[:, GROUP * slot:GROUP * slot + GROUP, TOKEN]
                pool.tensor_scalar(mine, mine, RING * GROUP * P, None, ALU.add).then_inc(s_token, 1)

            pool.wait_ge(s_tanh, 1)

            def step(u, c):
                if live(u, c - 2, GROUPS):
                    z_scale(u, c - 2)
                if live(u, c, GROUPS):
                    x_scale(u, c)
                if live(u, c - 2, GROUPS):
                    z_back(u, c - 2)
                if live(u, c - 6, GROUPS) and live(u, c - 2, GROUPS):
                    next_tokens(u, c - 6)
                if live(u, c - 5, GROUPS):
                    scatter(u, c - 5)

            for t in range(8):
                step(0, t)
            with pool.Fori(2, GROUPS // RING) as u:
                for c in range(RING):
                    step(u, c)
            for t in range(GROUPS, GROUPS + 5):
                step(0, t)

            def base_of(u, c):
                k, slot = RING * u + c, c % RING
                wait_reg(r_in[slot], 16 * (u + c // RING + 1))
                if after(u, c, RING):
                    wait_reg(s_res, k - RING + 1)
                    wait_reg(stored[slot], 16 * (u + c // RING))
                pool.tensor_copy(token[:, slot:slot + 1], srow_i[:, slot, TOKEN:TOKEN + 1]).then_inc(s_tok2, 1)
                pool.tensor_scalar(base[:, slot, :], srow[:, slot, 0:H], srow[:, slot, Z_SCALE:Z_SCALE + 1],
                                   srow[:, slot, MEAN:MEAN + 1], ALU.mult, ALU.add).then_inc(s_base, 1)

            def store(u, c):
                k, slot = RING * u + c, c % RING
                wait_reg(s_res, k + 1)
                wait_reg(s_tok2, k + 1)
                pool.indirect_dma_start(
                    out=out_rows, out_offset=bass.IndirectOffsetOnAxis(ap=token[:, slot:slot + 1], axis=0),
                    in_=res[:, slot, :], in_offset=None,
                    bounds_check=TOKENS - 1, oob_is_err=False).then_inc(stored[slot], 16)

            def step2(u, c):
                if live(u, c, TILES):
                    base_of(u, c)
                if live(u, c - 2, TILES):
                    store(u, c - 2)

            run_steps(pool, step2, TILES + 1, RING, TILES)
            for slot in range(RING):
                pool.wait_ge(stored[slot], 16 * (TILES // RING))

        @block.scalar
        def _(act):
            act.wait_ge(s_small, 16 * 7)
            act.activation(tanh_g[:, :], gates[:, :], ACT.Tanh).then_inc(s_tanh, 1)
            act.wait_ge(s_tanh, 1)
            act.wait_ge(s_woT, 1)
            act.activation(w_out_t[:, :], b_sc[:, 0:H], ACT.Copy, scale=tanh_g[:, 0:1]).then_inc(s_wo, 1)
            act.activation(bias_b[:, :], bias_raw[:, :], ACT.Copy, scale=tanh_g[:, 0:1]).then_inc(s_wo, 1)

            def copy_transposed(u, c):
                g = RING * u + c
                act.wait_ge(s_n1T_ps, g + 1)
                if after(u, c, 1):
                    act.wait_ge(s_sc, g)
                act.activation(n1T[:, :], b_n1T[:, :], ACT.Copy).then_inc(s_n1T, 1)
                act.wait_ge(s_ctxT_ps, g + 1)
                if after(u, c, 1):
                    act.wait_ge(s_val_ps, g)
                act.activation(ctxT[:, :], b_ctxT[:, 0:GROUP * K], ACT.Copy).then_inc(s_ctxT, 1)

            def affine(u, c):
                g = RING * u + c
                act.wait_ge(s_zT_ps, g + 1)
                if after(u, c, 1):
                    act.wait_ge(s_lg, g)
                act.activation(xfT[:, :], b_zT[:, :], ACT.Identity, bias=lnb[:, :], scale=lnw[:, :]).then_inc(s_xfT, 1)

            def copy_probs(u, c):
                g = RING * u + c
                act.wait_ge(s_pT_ps, g + 1)
                if after(u, c, 1):
                    act.wait_ge(s_att, g)
                act.activation(probsT[0:K, :], b_pT[0:K, :], ACT.Copy).then_inc(s_pT, 1)

            def softmax_exp(u, c):
                g = RING * u + c
                act.wait_ge(s_max, g + 1)
                if after(u, c, 1):
                    act.wait_ge(s_pT_ps, g)
                if after(u, c, 2):
                    act.wait_ge(s_inv, g - 1)
                for j in range(GROUP):
                    last = act.activation(probs[:, j, :], b_sc[:, j * K:(j + 1) * K], ACT.Exp,
                                          bias=neg_max[:, c % 2, j:j + 1],
                                          accum_out=row_sum[:, c % 2, j:j + 1])
                last.then_inc(s_prob, 1)

            def score_exp(u, c):
                p = 2 * u + c // 2
                act.wait_ge(s_lmax, p + 1)
                act.activation(exp_lg[:, :], lg_max[:, :], ACT.Exp, scale=-1.0).then_inc(s_elg, 1)

            def step(u, c):
                if live(u, c, GROUPS):
                    copy_transposed(u, c)
                if live(u, c - 2, GROUPS):
                    affine(u, c - 2)
                if live(u, c - 1, GROUPS):
                    copy_probs(u, c - 1)
                if live(u, c, GROUPS):
                    softmax_exp(u, c)
                if c % 2 == 0 and live(u, c - 4, GROUPS):
                    score_exp(u, c - 4)

            run_steps(act, step, GROUPS + 2, RING, GROUPS)

            act.wait_ge(s_big, 16 * 6)
            act.activation(down[:, :, :, :], down_raw[:, :, :, :], ACT.Copy, scale=tanh_g[:, 1:2]).then_inc(s_down, 1)

            def affine2(u, c):
                k = RING * u + c
                act.wait_ge(s_zT2_ps, k + 1)
                if after(u, c, 2):
                    act.wait_ge(s_gus, k - 1)
                act.activation(xfT2[:, c % 2], b_zT2[:, 0:P], ACT.Identity, bias=lnb[:, :],
                               scale=lnw[:, :]).then_inc(s_xfT2, 1)

            def silus(u, c):
                k, slot = RING * u + c, c % RING
                act.wait_ge(s_gur, k + 1)
                if after(u, c, 2):
                    act.wait_ge(s_hr, k - 1)
                act.activation(act_r[:, c % 2], b_gur[c % 2][:, 0:I], ACT.Silu,
                               scale=srow[:, slot, SCORE:SCORE + 1]).then_inc(s_ar, 1)
                act.wait_ge(s_gus, k + 1)
                if after(u, c, 2):
                    act.wait_ge(s_hs, k - 1)
                act.activation(act_s[:, c % 2], b_gus[c % 2][:, 0:I], ACT.Silu).then_inc(s_as, 1)

            def step2(u, c):
                if live(u, c, TILES):
                    affine2(u, c)
                if live(u, c - 1, TILES):
                    silus(u, c - 1)

            run_steps(act, step2, TILES, RING, TILES)

        @block.vector
        def _(dve):
            spare_reg = dve.alloc_register("spare_dve")
            dve.reg_mov(spare_reg, 0)

            def wait_reg(sem, count):
                if not isinstance(count, int):
                    count = dve.to_reg(count)
                    dve.wait_ge(s_const, CONSTS)
                dve.wait_ge(sem, count)

            def x_stats(u, c):
                g, slot = RING * u + c, c % RING
                dve.wait_ge(x_in[slot], 16 * (u + c // RING + 1))
                for j in range(GROUP):
                    last = dve.bn_stats(x_st[:, j, :], x_sb[:, slot, j, :])
                last.then_inc(s_xst, 1)
                wait_reg(s_xst, g + 1)
                for j in range(GROUP):
                    last = dve.bn_aggr(x_mv[:, j, :], x_st[:, j, :])
                last.then_inc(s_xmv, 1)

            def x_norm(u, c):
                g, slot = RING * u + c, c % RING
                dve.wait_ge(s_xrs, g + 1)
                if after(u, c, 2):
                    dve.wait_ge(s_n1T_ps, g - 1)
                for j in range(GROUP):
                    last = dve.tensor_scalar(n1[:, c % 2, j, :], x_sb[:, slot, j, :], x_mv[:, j, 0:1],
                                             x_rs[:, c % 2, j:j + 1], ALU.subtract, ALU.mult)
                last.then_inc(s_n1, 1)

            def score_max(u, c):
                g = RING * u + c
                dve.wait_ge(s_sc, g + 1)
                if after(u, c, 2):
                    dve.wait_ge(s_prob, g - 1)
                dve.tensor_reduce(neg_max[:, c % 2], b_sc[:, 0:GROUP * K].rearrange("p (j k) -> p j k", k=K),
                                  AX_X, ALU.max, negate=True).then_inc(s_max, 1)

            def value_bias(u, c):
                g = RING * u + c
                dve.wait_ge(s_val_ps, g + 1)
                if after(u, c, 2):
                    dve.wait_ge(s_att, g - 1)
                bias = bias_b[0:K, :].rearrange("p (a h) -> p a h", a=1).to_broadcast([K, GROUP, H])
                dve.tensor_tensor(vals[0:K, c % 2].rearrange("p (j h) -> p j h", h=H),
                                  b_val[0:K, :].rearrange("p (j h) -> p j h", h=H), bias, ALU.add).then_inc(s_val, 1)

            def residual(u, c):
                g, slot = RING * u + c, c % RING
                dve.wait_ge(s_prob, g + 1)
                dve.reciprocal(row_inv[:, :], row_sum[:, c % 2]).then_inc(s_inv, 1)
                dve.wait_ge(s_inv, g + 1)
                dve.wait_ge(s_att, g + 1)
                for j in range(GROUP):
                    last = dve.scalar_tensor_tensor(x1[:, j, :], b_att[:, j * H:(j + 1) * H], row_inv[:, j:j + 1],
                                                    x_sb[:, slot, j, :], ALU.mult, ALU.add)
                last.then_inc(s_x1, 1)
                dve.wait_ge(s_x1, g + 1)
                for j in range(GROUP):
                    last = dve.bn_stats(z_st[:, j, :], x1[:, j, :])
                last.then_inc(s_zst, 1)
                wait_reg(s_zst, g + 1)
                if after(u, c, RING):
                    wait_reg(sent[slot], 16 * GROUP * (u + c // RING))
                for j in range(GROUP):
                    last = dve.bn_aggr(rows[:, GROUP * slot + j, MEAN:VAR + 1], z_st[:, j, :])
                last.then_inc(s_zmv, 1)

            def z_norm(u, c):
                g, slot = RING * u + c, c % RING
                dve.wait_ge(s_zpw, g + 1)
                dve.wait_ge(s_zmv, g + 1)
                for j in range(GROUP):
                    at = GROUP * slot + j
                    last = dve.tensor_scalar(rows[:, at, 0:H], x1[:, j, :], rows[:, at, MEAN:MEAN + 1],
                                             z_pw[:, c % 2, 0, j:j + 1], ALU.subtract, ALU.mult)
                last.then_inc(s_z, 1)

            rev = expert_rev[:, :].rearrange("p (a e) -> p a e", a=1).to_broadcast([P, PT, E])

            def over_experts(v):
                return v.rearrange("p (t a) -> p t a", a=1).to_broadcast([P, PT, E])

            def choose(u, c):
                p = 2 * u + c // 2
                dve.wait_ge(s_lg, 2 * p + 2)
                dve.tensor_copy(lg[:, :, :], lg_ps).then_inc(s_lg_sb, 1)
                dve.wait_ge(s_lg_sb, p + 1)
                if after(u, c, 2):
                    dve.wait_ge(s_elg, p)
                dve.tensor_reduce(lg_max[:, :], lg[:, :, :], AX_X, ALU.max).then_inc(s_lmax, 1)
                dve.wait_ge(s_lmax, p + 1)
                dve.tensor_tensor(hit[:, :, :], lg[:, :, :], over_experts(lg_max[:, :]), ALU.is_equal).then_inc(s_hit, 1)
                dve.wait_ge(s_hit, p + 1)
                dve.tensor_tensor(hit_rev[:, :, :], hit[:, :, :], rev, ALU.mult).then_inc(s_rev, 1)
                dve.wait_ge(s_rev, p + 1)
                dve.tensor_reduce(best_rev[:, :], hit_rev[:, :, :], AX_X, ALU.max).then_inc(s_best, 1)
                dve.wait_ge(s_best, p + 1)
                if after(u, c, 2):
                    dve.wait_ge(s_rank, p)
                dve.tensor_tensor(onehot[:, 0:PT, :], rev, over_experts(best_rev[:, :]), ALU.is_equal).then_inc(s_hot, 1)

            def positions(u, c):
                p = 2 * u + c // 2
                dve.wait_ge(s_rank, p + 1)
                dve.wait_ge(s_free, p + 1)
                free = first_free[:, :].rearrange("p (a e) -> p a e", a=1).to_broadcast([P, PT, E])
                dve.tensor_tensor(place[:, :, :], rank_ps[:, 0:PT, :], free, ALU.add).then_inc(s_place, 1)
                dve.wait_ge(s_place, p + 1)
                dve.tensor_tensor(first_free[:, :], rank_ps[:, PT, :], first_free[:, :], ALU.add).then_inc(s_free, 1)
                dve.wait_ge(s_hot, p + 1)
                dve.tensor_tensor(place_hit[:, :, :], place[:, :, :], onehot[:, 0:PT, :], ALU.mult).then_inc(s_phit, 1)
                dve.wait_ge(s_elg, p + 1)
                dve.tensor_scalar(exp_lg1[:, :], exp_lg[:, :], 1.0, None, ALU.add).then_inc(s_elg1, 1)
                dve.wait_ge(s_phit, p + 1)
                dve.tensor_reduce(pos_f[:, :], place_hit[:, :, :], AX_X, ALU.add).then_inc(s_posf, 1)
                dve.wait_ge(s_elg1, p + 1)
                half = PT * ((c // 2) % 2)
                dve.reciprocal(rows[:, half:half + PT, SCORE], exp_lg1[:, :]).then_inc(s_score, 1)
                dve.wait_ge(s_posf, p + 1)
                if after(u, c, RING):
                    for s in (c % RING, (c + 1) % RING):
                        dve.wait_ge(sent[s], 16 * GROUP * (u + c // RING))
                dve.tensor_copy(pos[:, (c // 2) % 2, :], pos_f[:, :]).then_inc(s_pos, 1)

            dve.wait_ge(s_const, CONSTS)
            dve.wait_ge(s_wo, 2)

            def step(u, c):
                routed = c % 2 == 1 and live(u, c - 5, GROUPS)
                if routed:
                    choose(u, c - 5)
                if live(u, c - 1, GROUPS):
                    score_max(u, c - 1)
                    value_bias(u, c - 1)
                if live(u, c - 2, GROUPS):
                    residual(u, c - 2)
                if live(u, c, GROUPS):
                    x_stats(u, c)
                if routed:
                    positions(u, c - 5)
                if live(u, c - 2, GROUPS):
                    z_norm(u, c - 2)
                if live(u, c, GROUPS):
                    x_norm(u, c)

            for t in range(8):
                step(0, t)
            with dve.Fori(2, GROUPS // RING) as u:
                for c in range(RING):
                    step(u, c)
            for t in range(GROUPS, GROUPS + 4):
                step(0, t)

            made = [0]

            def link(ins):
                made[0] += 1
                ins.then_inc(s_tab, 1)
                dve.wait_ge(s_tab, made[0])

            NT = TOKENS // P
            dve.wait_ge(s_free, PAIRS + 1)
            link(dve.tensor_copy(fill_row[:, :], first_free[:, :]))
            link(dve.tensor_tensor(counts[:, :], first_free[:, :], region_at[:, :], ALU.subtract))
            link(dve.tensor_tensor(over[:, :, :], counts[:, :].rearrange("p (e a) -> p e a", a=1).to_broadcast([P, E, NT]),
                                   steps128[:, :].rearrange("p (a n) -> p a n", a=1).to_broadcast([P, E, NT]), ALU.is_gt))
            link(dve.tensor_reduce(n_tiles[:, :], over[:, :, :], AX_X, ALU.add))
            link(dve.tensor_copy(cum[:, 0, :], n_tiles[:, :]))
            for i, d in enumerate((1, 2, 4)):
                link(dve.tensor_copy(cum[:, i + 1, 0:d], cum[:, i, 0:d]))
                link(dve.tensor_tensor(cum[:, i + 1, d:E], cum[:, i, d:E], cum[:, i, 0:E - d], ALU.add))
            cums = cum[:, 3, :].rearrange("p (a e) -> p a e", a=1).to_broadcast([P, TILES, E])
            link(dve.tensor_tensor(past[:, :, :], tile_no[:, :].rearrange("p (t a) -> p t a", a=1).to_broadcast([P, TILES, E]),
                                   cums, ALU.is_ge))
            link(dve.tensor_reduce(tile_e[:, :], past[:, :, :], AX_X, ALU.add))
            link(dve.tensor_tensor(past_cum[:, :, :], past[:, :, :], cums, ALU.mult))
            link(dve.tensor_reduce(tile_c[:, :], past_cum[:, :, :], AX_X, ALU.max))
            link(dve.tensor_tensor(tile_a[:, :], tile_no[:, :], tile_c[:, :], ALU.subtract))
            link(dve.tensor_scalar(tile_b[:, :], tile_e[:, :], float(REGION), None, ALU.mult))
            link(dve.scalar_tensor_tensor(tile_c[:, :], tile_a[:, :], float(P), tile_b[:, :], ALU.mult, ALU.add))
            link(dve.tensor_scalar(tile_row[:, :], tile_c[:, :], float(E * REGION), None, ALU.min))
            link(dve.tensor_scalar(tile_expert[:, :], tile_e[:, :], float(E - 1), None, ALU.min))
            dve.engine_nop().then_inc(s_table, 1)

            def hiddenT(u, c):
                k = RING * u + c
                dve.wait_ge(s_hT_ps, k + 1)
                if after(u, c, 2):
                    dve.wait_ge(s_dn, k - 1)
                dve.tensor_copy(hidT_r[:, c % 2], b_hT[:, 0:I]).then_inc(s_hT, 1)

            def hidden(u, c):
                k, slot = RING * u + c, c % RING
                dve.wait_ge(s_ar, k + 1)
                if after(u, c, 2):
                    dve.wait_ge(s_hT_ps, k - 1)
                dve.scalar_tensor_tensor(hid_r[:, c % 2], b_gur[c % 2][:, I:2 * I], srow[:, slot, SCORE:SCORE + 1],
                                         act_r[:, c % 2], ALU.mult, ALU.mult).then_inc(s_hr, 1)
                dve.wait_ge(s_as, k + 1)
                if after(u, c, 2):
                    dve.wait_ge(s_dn, k - 1)
                dve.tensor_tensor(hid_s[:, c % 2], b_gus[c % 2][:, I:2 * I], act_s[:, c % 2], ALU.mult).then_inc(s_hs, 1)

            def result(u, c):
                k, slot = RING * u + c, c % RING
                dve.wait_ge(s_dn, k + 1)
                dve.wait_ge(s_base, k + 1)
                if after(u, c, RING):
                    dve.wait_ge(stored[slot], 16 * (u + c // RING))
                dve.tensor_tensor(res[:, slot, :], b_dn[c % 2][:, 0:H], base[:, slot, :], ALU.add).then_inc(s_res, 1)

            def step2(u, c):
                if live(u, c - 1, TILES):
                    hidden(u, c - 1)
                if live(u, c - 2, TILES):
                    hiddenT(u, c - 2)
                    result(u, c - 2)

            run_steps(dve, step2, TILES + 1, 2 * RING, TILES)

        @block.tensor
        def _(pe):
            pe.wait_ge(s_const, CONSTS)
            pe.wait_ge(s_small, 16 * 7)
            pe.transpose(b_sc[:, 0:H], w_out_sb[:, :], ident[:, :]).then_inc(s_woT, 1)
            pe.wait_ge(s_wo, 2)

            def transposes(u, c):
                g, slot = RING * u + c, c % RING
                pe.wait_ge(s_n1, g + 1)
                if after(u, c, 1):
                    pe.wait_ge(s_n1T, g)
                for j in range(GROUP):
                    last = pe.transpose(b_n1T[:, j * P:(j + 1) * P], n1[:, c % 2, j, :], ident[:, :])
                last.then_inc(s_n1T_ps, 1)
                pe.wait_ge(c_in[slot], 16 * (u + c // RING + 1))
                if after(u, c, 1):
                    pe.wait_ge(s_ctxT, g)
                for j in range(GROUP):
                    last = pe.transpose(b_ctxT[:, j * K:(j + 1) * K], ctx_sb[0:K, slot, j, :], ident[0:K, 0:K])
                last.then_inc(s_ctxT_ps, 1)

            def z_transposes(u, c):
                g, slot = RING * u + c, c % RING
                pe.wait_ge(s_z, g + 1)
                if after(u, c, 1):
                    pe.wait_ge(s_xfT, g)
                for j in range(GROUP):
                    last = pe.transpose(b_zT[:, j * P:(j + 1) * P], rows[:, GROUP * slot + j, 0:H], ident[:, :])
                last.then_inc(s_zT_ps, 1)

            def scores(u, c):
                g = RING * u + c
                pe.wait_ge(s_n1T, g + 1)
                pe.wait_ge(s_ctxT, g + 1)
                if after(u, c, 1):
                    pe.wait_ge(s_prob, g)
                for j in range(GROUP):
                    last = pe.matmul(b_sc[:, j * K:(j + 1) * K], n1T[:, j * P:(j + 1) * P],
                                     ctxT[:, j * K:(j + 1) * K], start=True, stop=True)
                last.then_inc(s_sc, 1)
                if after(u, c, 1):
                    pe.wait_ge(s_val, g)
                for j in range(GROUP):
                    last = pe.matmul(b_val[0:K, j * H:(j + 1) * H], ctxT[:, j * K:(j + 1) * K], w_out_t[:, :],
                                     start=True, stop=True)
                last.then_inc(s_val_ps, 1)

            def logits(u, c):
                g = RING * u + c
                p = 2 * u + c // 2
                pe.wait_ge(s_xfT, g + 1)
                if after(u, c, 2):
                    if c % 2 == 0:
                        pe.wait_ge(s_lg_sb, p)
                    else:
                        pe.wait_ge(s_free, p + 1)
                for j in range(GROUP):
                    last = pe.matmul(lg_ps[:, (c % 2) * GROUP + j, :], xfT[:, j * P:(j + 1) * P], router[:, :],
                                     start=True, stop=True)
                last.then_inc(s_lg, 1)

            def probs_transposes(u, c):
                g = RING * u + c
                pe.wait_ge(s_prob, g + 1)
                if after(u, c, 1):
                    pe.wait_ge(s_pT, g)
                for j in range(GROUP):
                    last = pe.transpose(b_pT[0:K, j * P:(j + 1) * P], probs[:, j, :], ident[:, :])
                last.then_inc(s_pT_ps, 1)

            def attend(u, c):
                g = RING * u + c
                pe.wait_ge(s_pT, g + 1)
                pe.wait_ge(s_val, g + 1)
                if after(u, c, 1):
                    pe.wait_ge(s_x1, g)
                for j in range(GROUP):
                    last = pe.matmul(b_att[:, j * H:(j + 1) * H], probsT[0:K, j * P:(j + 1) * P],
                                     vals[0:K, c % 2, j * H:(j + 1) * H], start=True, stop=True)
                last.then_inc(s_att, 1)

            def ranks(u, c):
                p = 2 * u + c // 2
                pe.wait_ge(s_hot, p + 1)
                pe.wait_ge(s_free, p + 1)
                pe.matmul(rank_ps, before[:, :], onehot[:, :, :], start=True, stop=False)
                for t in range(PT):
                    later = PT - t
                    last = pe.matmul(rank_ps[:, t + 1:PT + 1, :], ones[:, :],
                                     onehot[:, t:t + 1, :].to_broadcast([P, later, E]),
                                     start=False, stop=(t == PT - 1))
                last.then_inc(s_rank, 1)

            def step(u, c):
                if live(u, c, GROUPS):
                    transposes(u, c)
                if live(u, c - 2, GROUPS):
                    z_transposes(u, c - 2)
                if live(u, c, GROUPS):
                    scores(u, c)
                if live(u, c - 2, GROUPS):
                    logits(u, c - 2)
                if live(u, c - 1, GROUPS):
                    probs_transposes(u, c - 1)
                    attend(u, c - 1)
                if c % 2 == 0 and live(u, c - 4, GROUPS):
                    ranks(u, c - 4)

            run_steps(pe, step, GROUPS + 2, RING, GROUPS)

            pe.wait_ge(s_table, 1)
            pe.wait_ge(s_big, 16 * 6)
            pe.wait_ge(s_down, 1)
            pe.wait_ge(s_free, PAIRS + 1)

            def z_transpose(u, c):
                k, slot = RING * u + c, c % RING
                pe.wait_ge(r_in[slot], 16 * (u + c // RING + 1))
                if after(u, c, 1):
                    pe.wait_ge(s_xfT2, k)
                pe.transpose(b_zT2[:, 0:P], srow[:, slot, 0:H], ident[:, :]).then_inc(s_zT2_ps, 1)

            def gate_and_up(u, c):
                k = RING * u + c
                expert = pe.value_load(tile_expert[0:1, bass.ds(k, 1)], min_val=0, max_val=E - 1)
                pe.wait_ge(s_xfT2, k + 1)
                if after(u, c, 2):
                    pe.wait_ge(s_hr, k - 1)
                xf = xfT2[:, c % 2]
                pe.matmul(b_gur[c % 2][:, :], xf, gate_up[:, bass.ds(expert, 1), :].rearrange("p a n -> p (a n)"),
                          start=True, stop=True).then_inc(s_gur, 1)
                if after(u, c, 2):
                    pe.wait_ge(s_hs, k - 1)
                for n in range(2 * CHUNKS):
                    last = pe.matmul(b_gus[c % 2][:, n * P:(n + 1) * P], sh_gu[:, n * P:(n + 1) * P], xf,
                                     start=True, stop=True)
                last.then_inc(s_gus, 1)

            def hidden_transposes(u, c):
                k = RING * u + c
                pe.wait_ge(s_hr, k + 1)
                if after(u, c, 1):
                    pe.wait_ge(s_hT, k)
                for n in range(CHUNKS):
                    last = pe.transpose(b_hT[:, n * P:(n + 1) * P], hid_r[:, c % 2, n * P:(n + 1) * P], ident[:, :])
                last.then_inc(s_hT_ps, 1)

            def down_products(u, c):
                k = RING * u + c
                expert = pe.value_load(tile_expert[0:1, bass.ds(k, 1)], min_val=0, max_val=E - 1)
                pe.wait_ge(s_hs, k + 1)
                if after(u, c, 2):
                    pe.wait_ge(s_res, k - 1)
                for n in range(CHUNKS):
                    pe.matmul(b_dn[c % 2][:, 0:H], hid_s[:, c % 2, n * P:(n + 1) * P], down[:, E, n, :],
                              start=(n == 0), stop=False)
                pe.wait_ge(s_hT, k + 1)
                for n in range(CHUNKS):
                    last = pe.matmul(b_dn[c % 2][:, 0:H], hidT_r[:, c % 2, n * P:(n + 1) * P],
                                     down[:, bass.ds(expert, 1), n, :].rearrange("p a n -> p (a n)"),
                                     start=False, stop=(n == CHUNKS - 1))
                last.then_inc(s_dn, 1)

            def step2(u, c):
                if live(u, c, TILES):
                    z_transpose(u, c)
                if live(u, c - 1, TILES):
                    gate_and_up(u, c - 1)
                if live(u, c - 2, TILES):
                    hidden_transposes(u, c - 2)
                    down_products(u, c - 2)

            run_steps(pe, step2, TILES + 1, RING, TILES)


_INS = ["x", "ctx_1024", "g_xattn", "g_ffn", "L0_xattn_W_out", "L0_xattn_b_out", "L0_ffn_ln_w", "L0_ffn_ln_b",
        "L0_ffn_router_w", "L0_ffn_gate_w", "L0_ffn_up_w", "L0_ffn_down_w", "L0_ffn_sh_gate", "L0_ffn_sh_up",
        "L0_ffn_sh_down"]


def kernel(**inputs):
    import numpy as np
    import concourse.bacc as bacc
    from concourse import mybir as mb
    from concourse.bass_utils import run_bass_kernel_spmd

    nc = bacc.Bacc("TRN2", target_bir_lowering=False, num_devices=1)
    arrays, args = {}, []
    for name in _INS:
        a = np.ascontiguousarray(inputs[name])
        arrays[f"in_{name}"] = a
        args.append(nc.dram_tensor(f"in_{name}", a.shape, mb.dt.from_np(a.dtype), kind="ExternalInput").ap())
    shape = tuple(inputs["x"].shape)
    args.append(nc.dram_tensor("out_0", shape, mb.dt.float32, kind="ExternalOutput").ap())
    flamingo_kernel(nc, *args)
    r = run_bass_kernel_spmd(nc, [arrays], core_ids=[0])
    return r.results[0]["out_0"]
```

```python
from contextlib import ExitStack

import concourse.bass as bass
from concourse import mybir

ALU = mybir.AluOpType
ACT = mybir.ActivationFunctionType
F32 = mybir.dt.float32
BF16 = mybir.dt.bfloat16
I32 = mybir.dt.int32
AX_X = mybir.AxisListType.X

P = 128
EPS = 1e-5
GROUP = 4
RING = 4


def flamingo_kernel(nc, x, ctx_in, g_xattn, g_ffn, w_out, b_out, ln_w, ln_b, router_w,
                    gate_w, up_w, down_w, sh_gate, sh_up, sh_down, out):
    B, S, H = x.shape
    K = ctx_in.shape[1]
    E, _, I = gate_w.shape
    assert S == P and H == P and B % (GROUP * RING) == 0 and I == 2 * P
    GROUPS = B // GROUP
    PAIRS = GROUPS // 2
    PT = 2 * GROUP
    TOKENS = B * S
    CHUNKS = I // P
    REGION = TOKENS + P
    TILES = TOKENS // P + E
    assert TILES % RING == 0
    Z_SCALE, MEAN, SCORE, TOKEN = H, H + 1, H + 2, H + 3
    ROW = H + 4
    NO_TOKEN = 1 << 20
    CONSTS = 9

    scratch = nc.dram_tensor("sorted_rows", [E * REGION + P, ROW], F32).ap()
    out_rows = out.rearrange("b s h -> (b s) h")
    x_v = x.rearrange("b s h -> s b h")
    ctx_v = ctx_in.rearrange("b k h -> k b h")

    with ExitStack() as stack:
        def sb(name, shape, dt=F32):
            return stack.enter_context(nc.sbuf_tensor(name, shape, dt))

        def sem(name):
            return stack.enter_context(nc.semaphore(name))

        banks = [stack.enter_context(nc.psum_tensor(f"bank{i}", [P, 512], F32)) for i in range(8)]

        ident = sb("ident", [P, P])
        ones = sb("ones", [P, P], BF16)
        before = sb("before", [P, P], BF16)
        expert_rev = sb("expert_rev", [P, E])
        gates = sb("gates", [P, 2])
        tanh_g = sb("tanh_g", [P, 2])
        w_out_sb = sb("w_out_sb", [P, H])
        w_out_t = sb("w_out_t", [P, H])
        bias_raw = sb("bias_raw", [P, H])
        bias_b = sb("bias_b", [P, H])
        lnw = sb("lnw", [P, 1])
        lnb = sb("lnb", [P, 1])
        router = sb("router", [P, E])
        gate_up = sb("gate_up", [P, E, 2 * I])
        down_raw = sb("down_raw", [P, E + 1, CHUNKS, H])
        down = sb("down", [P, E + 1, CHUNKS, H])
        sh_gu = sb("sh_gu", [P, 2 * I])

        x_sb = sb("x_sb", [P, RING, GROUP, H])
        ctx_sb = sb("ctx_sb", [P, RING, GROUP, H])
        x_st = sb("x_st", [P, GROUP, 6])
        x_mv = sb("x_mv", [P, 2, GROUP, 2])
        z_mv = sb("z_mv", [P, 2, GROUP, 2])
        sq = sb("sq", [P, 2, 3, GROUP])
        ln_sq = sb("ln_sq", [P, 3, GROUP])
        root0 = sb("root0", [P, 3, GROUP])
        root0_2 = sb("root0_2", [P, 3, GROUP])
        root_err = sb("root_err", [P, 3, GROUP])
        root = sb("root", [P, 2, 3, GROUP])
        x_bias = sb("x_bias", [P, 2, GROUP])
        z_bias = sb("z_bias", [P, 2, GROUP])
        z_len = sb("z_len", [P, GROUP])
        n1 = sb("n1", [P, 2, GROUP, H])
        n1T = sb("n1T", [P, GROUP * P])
        ctxT = sb("ctxT", [P, GROUP * K])
        neg_max = sb("neg_max", [P, 2, GROUP])
        probs = sb("probs", [P, GROUP, K])
        row_sum = sb("row_sum", [P, 2, GROUP])
        row_inv = sb("row_inv", [P, GROUP])
        probsT = sb("probsT", [P, GROUP * P])
        vals = sb("vals", [P, 2, GROUP * H])
        x1 = sb("x1", [P, 2, GROUP, H])
        z_st = sb("z_st", [P, GROUP, 6])
        z_t = sb("z_t", [P, GROUP])
        rows = sb("rows", [P, RING * GROUP, ROW])
        rows_i = rows[:, :, :].bitcast(I32)
        xfT = sb("xfT", [P, GROUP * P])
        lg = sb("lg", [P, PT, E])
        lg_max = sb("lg_max", [P, PT])
        hit = sb("hit", [P, PT, E])
        hit_rev = sb("hit_rev", [P, PT, E])
        best_rev = sb("best_rev", [P, PT])
        onehot = sb("onehot", [P, PT + 1, E], BF16)
        place = sb("place", [P, PT, E])
        place_hit = sb("place_hit", [P, PT, E])
        pos_f = sb("pos_f", [P, PT])
        pos = sb("pos", [P, 2, PT], I32)
        first_free = sb("first_free", [P, E])
        exp_lg = sb("exp_lg", [P, PT])
        exp_lg1 = sb("exp_lg1", [P, PT])

        region_at = sb("region_at", [P, E])
        counts = sb("counts", [P, E])
        steps128 = sb("steps128", [P, TOKENS // P])
        over = sb("over", [P, E, TOKENS // P])
        n_tiles = sb("n_tiles", [P, E])
        cum = sb("cum", [P, 4, E])
        tile_no = sb("tile_no", [P, TILES])
        past = sb("past", [P, TILES, E])
        past_cum = sb("past_cum", [P, TILES, E])
        tile_e = sb("tile_e", [P, TILES])
        tile_c = sb("tile_c", [P, TILES])
        tile_a = sb("tile_a", [P, TILES])
        tile_b = sb("tile_b", [P, TILES])
        tile_row = sb("tile_row", [P, TILES], I32)
        tile_expert = sb("tile_expert", [P, TILES], I32)
        fill_row = sb("fill_row", [P, E], I32)
        filling = sb("filling", [P, ROW])
        filling_i = filling[:, :].bitcast(I32)

        srow = sb("srow", [P, RING, ROW])
        srow_i = srow[:, :, :].bitcast(I32)
        token = sb("token", [P, RING], I32)
        base = sb("base", [P, RING, H])
        xfT2 = sb("xfT2", [P, 2, P])
        act_r = sb("act_r", [P, 2, I])
        act_s = sb("act_s", [P, 2, I])
        hid_r = sb("hid_r", [P, 2, I])
        hid_s = sb("hid_s", [P, 2, I])
        hidT_r = sb("hidT_r", [P, 2, I])
        res = sb("res", [P, RING, H])

        s_const = sem("s_const")
        s_const0 = sem("s_const0")
        s_small = sem("s_small")
        s_big = sem("s_big")
        s_tanh = sem("s_tanh")
        s_woT = sem("s_woT")
        s_wo = sem("s_wo")
        s_down = sem("s_down")
        x_in = [sem(f"x_in{i}") for i in range(RING)]
        c_in = [sem(f"c_in{i}") for i in range(RING)]
        s_xst, s_xmv, s_xsq = sem("s_xst"), sem("s_xmv"), sem("s_xsq")
        s_xb = sem("s_xb")
        s_lnsq, s_root0, s_root02, s_rerr, s_root = sem("s_lnsq"), sem("s_root0"), sem("s_root02"), sem("s_rerr"), sem("s_root")
        s_n1 = sem("s_n1")
        s_n1T_ps, s_ctxT_ps, s_n1T, s_ctxT = sem("s_n1T_ps"), sem("s_ctxT_ps"), sem("s_n1T"), sem("s_ctxT")
        s_sc, s_val_ps, s_val = sem("s_sc"), sem("s_val_ps"), sem("s_val")
        s_max, s_prob = sem("s_max"), sem("s_prob")
        s_pT_ps, s_pT, s_att = sem("s_pT_ps"), sem("s_pT"), sem("s_att")
        s_inv, s_x1, s_zst, s_zmv = sem("s_inv"), sem("s_x1"), sem("s_zst"), sem("s_zmv")
        s_zsq, s_zb, s_zlen, s_zt, s_zsc = sem("s_zsq"), sem("s_zb"), sem("s_zlen"), sem("s_zt"), sem("s_zsc")
        s_z, s_zT_ps, s_xfT, s_lg = sem("s_z"), sem("s_zT_ps"), sem("s_xfT"), sem("s_lg")
        s_lg_sb, s_lmax, s_hit, s_rev, s_best = sem("s_lg_sb"), sem("s_lmax"), sem("s_hit"), sem("s_rev"), sem("s_best")
        s_hot, s_rank, s_place, s_phit = sem("s_hot"), sem("s_rank"), sem("s_place"), sem("s_phit")
        s_free, s_posf, s_pos = sem("s_free"), sem("s_posf"), sem("s_pos")
        s_elg, s_elg1, s_score, s_token = sem("s_elg"), sem("s_elg1"), sem("s_score"), sem("s_token")
        sent = [sem(f"sent{i}") for i in range(RING)]
        s_tab = sem("s_tab")
        s_table = sem("s_table")
        s_fill = sem("s_fill")
        r_in = [sem(f"r_in{i}") for i in range(RING)]
        s_tok2, s_base = sem("s_tok2"), sem("s_base")
        s_zT2_ps, s_xfT2 = sem("s_zT2_ps"), sem("s_xfT2")
        s_gur, s_gus, s_ar, s_as = sem("s_gur"), sem("s_gus"), sem("s_ar"), sem("s_as")
        s_hr, s_hs, s_hT_ps, s_hT = sem("s_hr"), sem("s_hs"), sem("s_hT_ps"), sem("s_hT")
        s_dn, s_res = sem("s_dn"), sem("s_res")
        stored = [sem(f"stored{i}") for i in range(RING)]

        b_n1T, b_ctxT, b_sc, b_val, b_pT, b_att, b_zT, b_lg = banks
        lg_ps = b_lg[:, 0:PT * E].rearrange("p (t e) -> p t e", e=E)
        rank_ps = b_lg[:, 128:128 + (PT + 1) * E].rearrange("p (t e) -> p t e", e=E)
        b_zT2, b_hT = banks[0], banks[1]
        b_gur, b_gus, b_dn = banks[2:4], banks[4:6], banks[6:8]

        def after(u, c, least):
            return not isinstance(u, int) or RING * u + c >= least

        def run_steps(eng, step, last, first_looped, end_looped):
            for t in range(first_looped):
                step(0, t)
            with eng.Fori(first_looped // RING, end_looped // RING) as u:
                for c in range(RING):
                    step(u, c)
            for t in range(end_looped, last + 1):
                step(0, t)

        def live(u, c, count):
            return not isinstance(u, int) or 0 <= RING * u + c < count

        block = stack.enter_context(nc.Block())

        @block.sync
        def _(sp):
            def load_group(u, c):
                g, slot = RING * u + c, c % RING
                if after(u, c, RING):
                    sp.wait_ge(s_x1, g - RING + 1)
                sp.dma_start(x_sb[:, slot], x_v[:, bass.ds(g * GROUP, GROUP), :]).then_inc(x_in[slot], 16)
                if after(u, c, RING):
                    sp.wait_ge(s_ctxT_ps, g - RING + 1)
                sp.dma_start(ctx_sb[0:K, slot], ctx_v[:, bass.ds(g * GROUP, GROUP), :]).then_inc(c_in[slot], 16)

            load_group(0, 0)
            sp.dma_start(w_out_sb[:, :], w_out).then_inc(s_small, 16)
            sp.dma_start(bias_raw[:, :], b_out.rearrange("(a h) -> a h", a=1).to_broadcast([P, H])).then_inc(s_small, 16)
            sp.dma_start(gates[:, 0:1], g_xattn.rearrange("(a h) -> a h", a=1).to_broadcast([P, 1])).then_inc(s_small, 16)
            sp.dma_start(gates[:, 1:2], g_ffn.rearrange("(a h) -> a h", a=1).to_broadcast([P, 1])).then_inc(s_small, 16)
            sp.dma_start(lnw[:, :], ln_w.rearrange("(h a) -> h a", a=1)).then_inc(s_small, 16)
            sp.dma_start(lnb[:, :], ln_b.rearrange("(h a) -> h a", a=1)).then_inc(s_small, 16)
            sp.dma_start(router[:, :], router_w).then_inc(s_small, 16)
            for c in range(1, RING):
                load_group(0, c)
            sp.dma_start(down_raw[:, 0:E], down_w.rearrange("e (c p) h -> p e c h", p=P)).then_inc(s_big, 16)
            sp.dma_start(down_raw[:, E], sh_down.rearrange("(c p) h -> p c h", p=P)).then_inc(s_big, 16)
            sp.dma_start(gate_up[:, :, 0:I], gate_w.rearrange("e h i -> h e i")).then_inc(s_big, 16)
            sp.dma_start(gate_up[:, :, I:2 * I], up_w.rearrange("e h i -> h e i")).then_inc(s_big, 16)
            sp.dma_start(sh_gu[:, 0:I], sh_gate).then_inc(s_big, 16)
            sp.dma_start(sh_gu[:, I:2 * I], sh_up).then_inc(s_big, 16)
            with sp.Fori(1, GROUPS // RING) as u:
                for c in range(RING):
                    load_group(u, c)

            sp.wait_ge(s_table, 1)
            for e in range(E):
                at = sp.value_load(fill_row[0:1, e:e + 1], min_val=0, max_val=E * REGION)
                sp.dma_start(scratch[bass.ds(at, P), :], filling[:, :]).then_inc(s_fill, 16)
            sp.dma_start(scratch[E * REGION:E * REGION + P, :], filling[:, :]).then_inc(s_fill, 16)
            sp.wait_ge(s_fill, 16 * (E + 1))
            for slot in range(RING):
                sp.wait_ge(sent[slot], 16 * GROUP * (GROUPS // RING))

            def load_tile(u, c):
                k, slot = RING * u + c, c % RING
                if after(u, c, RING):
                    sp.wait_ge(s_base, k - RING + 1)
                    sp.wait_ge(s_zT2_ps, k - RING + 1)
                    sp.wait_ge(s_hr, k - RING + 1)
                at = sp.value_load(tile_row[0:1, bass.ds(k, 1)], min_val=0, max_val=E * REGION)
                sp.dma_start(srow[:, slot], scratch[bass.ds(at, P), :]).then_inc(r_in[slot], 16)

            for c in range(RING):
                load_tile(0, c)
            with sp.Fori(1, TILES // RING) as u:
                for c in range(RING):
                    load_tile(u, c)

        @block.gpsimd
        def _(pool):
            pool.memset(ident[:, :], 0.0).then_inc(s_const0, 1)
            pool.memset(before[:, :], 1.0).then_inc(s_const0, 1)
            pool.memset(ones[:, :], 1.0).then_inc(s_const, 1)
            pool.memset(onehot[:, :, :], 0.0).then_inc(s_const, 1)
            pool.memset(filling[:, :], 0.0).then_inc(s_const0, 1)
            pool.wait_ge(s_const0, 3)
            pool.affine_select(out=ident[:, :], in_=ident[:, :], compare_op=ALU.not_equal, fill=1.0,
                               base=0, pattern=[[-1, P]], channel_multiplier=1).then_inc(s_const, 1)
            pool.affine_select(out=before[:, :], in_=before[:, :], compare_op=ALU.is_gt, fill=0.0,
                               base=0, pattern=[[1, P]], channel_multiplier=-1).then_inc(s_const, 1)
            pool.memset(filling_i[:, TOKEN:TOKEN + 1], NO_TOKEN).then_inc(s_const, 1)
            pool.iota(expert_rev[:, :], pattern=[[-1, E]], base=E, channel_multiplier=0,
                      allow_small_or_imprecise_dtypes=True).then_inc(s_const, 1)
            pool.iota(first_free[:, :], pattern=[[REGION, E]], base=0, channel_multiplier=0,
                      allow_small_or_imprecise_dtypes=True).then_inc(s_free, 1)
            pool.iota(region_at[:, :], pattern=[[REGION, E]], base=0, channel_multiplier=0,
                      allow_small_or_imprecise_dtypes=True).then_inc(s_const, 1)
            pool.iota(steps128[:, :], pattern=[[P, TOKENS // P]], base=0, channel_multiplier=0,
                      allow_small_or_imprecise_dtypes=True).then_inc(s_const, 1)
            pool.iota(tile_no[:, :], pattern=[[1, TILES]], base=0, channel_multiplier=0,
                      allow_small_or_imprecise_dtypes=True).then_inc(s_const, 1)
            pool.iota(rows_i[:, :, TOKEN:TOKEN + 1], pattern=[[P, RING * GROUP], [0, 1]], base=0,
                      channel_multiplier=1).then_inc(s_token, RING)
            pool.wait_ge(s_const, CONSTS)
            spare_reg = pool.alloc_register("spare_pool")
            pool.reg_mov(spare_reg, 0)

            def wait_reg(sem, count):
                if not isinstance(count, int):
                    count = pool.to_reg(count)
                    pool.wait_ge(s_const, CONSTS)
                pool.wait_ge(sem, count)

            def x_norm(u, c):
                g, slot = RING * u + c, c % RING
                wait_reg(s_xb, g + 1)
                if after(u, c, 2):
                    wait_reg(s_n1T_ps, g - 1)
                for j in range(GROUP):
                    last = pool.tensor_scalar(n1[:, c % 2, j, :], x_sb[:, slot, j, :], root[:, c % 2, 0, j:j + 1],
                                              x_bias[:, c % 2, j:j + 1], ALU.mult, ALU.add)
                last.then_inc(s_n1, 1)

            def scatter(u, c):
                g, slot = RING * u + c, c % RING
                p = 2 * u + c // 2
                wait_reg(s_pos, p + 1)
                wait_reg(s_score, p + 1)
                wait_reg(s_zsc, g + 1)
                wait_reg(s_z, g + 1)
                wait_reg(s_token, g + 1)
                for j in range(GROUP):
                    pool.indirect_dma_start(
                        out=scratch, out_offset=bass.IndirectOffsetOnAxis(
                            ap=pos[:, (c // 2) % 2, (c % 2) * GROUP + j:(c % 2) * GROUP + j + 1], axis=0),
                        in_=rows[:, GROUP * slot + j, :], in_offset=None).then_inc(sent[slot], 16)

            def next_tokens(u, c):
                g, slot = RING * u + c, c % RING
                wait_reg(sent[slot], 16 * GROUP * (u + c // RING + 1))
                mine = rows_i[:, GROUP * slot:GROUP * slot + GROUP, TOKEN]
                pool.tensor_scalar(mine, mine, RING * GROUP * P, None, ALU.add).then_inc(s_token, 1)

            def step(u, c):
                if live(u, c, GROUPS):
                    x_norm(u, c)
                if live(u, c - 6, GROUPS):
                    scatter(u, c - 6)
                if live(u, c - 8, GROUPS - RING):
                    next_tokens(u, c - 8)

            run_steps(pool, step, GROUPS + 5, 2 * RING, GROUPS)

            def base_of(u, c):
                k, slot = RING * u + c, c % RING
                wait_reg(r_in[slot], 16 * (u + c // RING + 1))
                if after(u, c, RING):
                    wait_reg(s_res, k - RING + 1)
                    wait_reg(stored[slot], 16 * (u + c // RING))
                pool.tensor_copy(token[:, slot:slot + 1], srow_i[:, slot, TOKEN:TOKEN + 1]).then_inc(s_tok2, 1)
                pool.tensor_scalar(base[:, slot, :], srow[:, slot, 0:H], srow[:, slot, Z_SCALE:Z_SCALE + 1],
                                   srow[:, slot, MEAN:MEAN + 1], ALU.mult, ALU.add).then_inc(s_base, 1)

            def store(u, c):
                k, slot = RING * u + c, c % RING
                wait_reg(s_res, k + 1)
                wait_reg(s_tok2, k + 1)
                pool.indirect_dma_start(
                    out=out_rows, out_offset=bass.IndirectOffsetOnAxis(ap=token[:, slot:slot + 1], axis=0),
                    in_=res[:, slot, :], in_offset=None,
                    bounds_check=TOKENS - 1, oob_is_err=False).then_inc(stored[slot], 16)

            def step2(u, c):
                if live(u, c, TILES):
                    base_of(u, c)
                if live(u, c - 2, TILES):
                    store(u, c - 2)

            run_steps(pool, step2, TILES + 1, RING, TILES)
            for slot in range(RING):
                pool.wait_ge(stored[slot], 16 * (TILES // RING))

        @block.scalar
        def _(act):
            act.wait_ge(s_small, 16 * 7)
            act.activation(tanh_g[:, :], gates[:, :], ACT.Tanh).then_inc(s_tanh, 1)
            act.wait_ge(s_tanh, 1)
            act.preload_act_table_set("natural_log_exp_and_others")
            act.wait_ge(s_woT, 1)
            act.activation(w_out_t[:, :], b_sc[:, 0:H], ACT.Copy, scale=tanh_g[:, 0:1]).then_inc(s_wo, 1)
            act.activation(bias_b[:, :], bias_raw[:, :], ACT.Copy, scale=tanh_g[:, 0:1]).then_inc(s_wo, 1)

            def copy_transposed(u, c):
                g = RING * u + c
                act.wait_ge(s_n1T_ps, g + 1)
                if after(u, c, 1):
                    act.wait_ge(s_sc, g)
                act.activation(n1T[:, :], b_n1T[:, :], ACT.Copy).then_inc(s_n1T, 1)
                act.wait_ge(s_ctxT_ps, g + 1)
                if after(u, c, 1):
                    act.wait_ge(s_val_ps, g)
                act.activation(ctxT[:, :], b_ctxT[:, 0:GROUP * K], ACT.Copy).then_inc(s_ctxT, 1)

            def affine(u, c):
                g = RING * u + c
                act.wait_ge(s_zT_ps, g + 1)
                if after(u, c, 1):
                    act.wait_ge(s_lg, g)
                act.activation(xfT[:, :], b_zT[:, :], ACT.Identity, bias=lnb[:, :], scale=lnw[:, :]).then_inc(s_xfT, 1)

            def copy_probs(u, c):
                g = RING * u + c
                act.wait_ge(s_pT_ps, g + 1)
                if after(u, c, 1):
                    act.wait_ge(s_att, g)
                act.activation(probsT[0:K, :], b_pT[0:K, :], ACT.Copy).then_inc(s_pT, 1)

            def softmax_exp(u, c):
                g = RING * u + c
                act.wait_ge(s_max, g + 1)
                if after(u, c, 1):
                    act.wait_ge(s_pT_ps, g)
                if after(u, c, 2):
                    act.wait_ge(s_inv, g - 1)
                for j in range(GROUP):
                    last = act.activation(probs[:, j, :], b_sc[:, j * K:(j + 1) * K], ACT.Exp,
                                          bias=neg_max[:, c % 2, j:j + 1],
                                          accum_out=row_sum[:, c % 2, j:j + 1])
                last.then_inc(s_prob, 1)

            def score_exp(u, c):
                p = 2 * u + c // 2
                act.wait_ge(s_lmax, p + 1)
                act.activation(exp_lg[:, :], lg_max[:, :], ACT.Exp, scale=-1.0).then_inc(s_elg, 1)

            def first_roots(u, c, lo, hi):
                act.wait_ge(s_xsq if hi == 1 else s_zsq, RING * u + c + 1 if hi == 1 else RING * u + c - 2)
                act.activation(ln_sq[:, lo:hi, :], sq[:, c % 2, lo:hi, :], ACT.Ln).then_inc(s_lnsq, 1)
                act.wait_ge(s_lnsq, RING * u + c + 1)
                act.activation(root0[:, lo:hi, :], ln_sq[:, lo:hi, :], ACT.Exp, scale=-0.5).then_inc(s_root0, 1)

            def z_norm(u, c):
                g, slot = RING * u + c, c % RING
                act.wait_ge(s_zb, g + 1)
                if after(u, c, RING):
                    act.wait_ge(sent[slot], 16 * GROUP * (u + c // RING))
                for j in range(GROUP):
                    last = act.activation(rows[:, GROUP * slot + j, 0:H], x1[:, c % 2, j, :], ACT.Identity,
                                          bias=z_bias[:, c % 2, j:j + 1], scale=root[:, (c + 1) % 2, 1, j:j + 1])
                last.then_inc(s_z, 1)

            def step(u, c):
                if live(u, c - 1, GROUPS):
                    copy_transposed(u, c - 1)
                if c % 2 == 0 and live(u, c - 6, GROUPS):
                    score_exp(u, c - 6)
                if live(u, c - 2, GROUPS):
                    copy_probs(u, c - 2)
                if live(u, c - 4, GROUPS):
                    affine(u, c - 4)
                lo, hi = (0 if live(u, c, GROUPS) else 1), (3 if live(u, c - 3, GROUPS) else 1)
                if lo < hi:
                    first_roots(u, c, lo, hi)
                if live(u, c - 1, GROUPS):
                    softmax_exp(u, c - 1)
                if live(u, c - 3, GROUPS):
                    z_norm(u, c - 3)

            run_steps(act, step, GROUPS + 4, 2 * RING, GROUPS)

            act.wait_ge(s_big, 16 * 6)
            act.activation(down[:, :, :, :], down_raw[:, :, :, :], ACT.Copy, scale=tanh_g[:, 1:2]).then_inc(s_down, 1)

            def affine2(u, c):
                k = RING * u + c
                act.wait_ge(s_zT2_ps, k + 1)
                if after(u, c, 2):
                    act.wait_ge(s_gus, k - 1)
                act.activation(xfT2[:, c % 2], b_zT2[:, 0:P], ACT.Identity, bias=lnb[:, :],
                               scale=lnw[:, :]).then_inc(s_xfT2, 1)

            def silus(u, c):
                k, slot = RING * u + c, c % RING
                act.wait_ge(s_gur, k + 1)
                if after(u, c, 2):
                    act.wait_ge(s_hr, k - 1)
                act.activation(act_r[:, c % 2], b_gur[c % 2][:, 0:I], ACT.Silu,
                               scale=srow[:, slot, SCORE:SCORE + 1]).then_inc(s_ar, 1)
                act.wait_ge(s_gus, k + 1)
                if after(u, c, 2):
                    act.wait_ge(s_hs, k - 1)
                act.activation(act_s[:, c % 2], b_gus[c % 2][:, 0:I], ACT.Silu).then_inc(s_as, 1)

            def step2(u, c):
                if live(u, c - 1, TILES):
                    silus(u, c - 1)
                if live(u, c, TILES):
                    affine2(u, c)

            run_steps(act, step2, TILES, RING, TILES)

        @block.vector
        def _(dve):
            spare_reg = dve.alloc_register("spare_dve")
            dve.reg_mov(spare_reg, 0)

            def wait_reg(sem, count):
                if not isinstance(count, int):
                    count = dve.to_reg(count)
                    dve.wait_ge(s_const, CONSTS)
                dve.wait_ge(sem, count)

            def x_stats(u, c):
                g, slot = RING * u + c, c % RING
                dve.wait_ge(x_in[slot], 16 * (u + c // RING + 1))
                if after(u, c, 2):
                    dve.wait_ge(s_n1, g - 1)
                for j in range(GROUP):
                    last = dve.bn_stats(x_st[:, j, :], x_sb[:, slot, j, :])
                last.then_inc(s_xst, 1)
                wait_reg(s_xst, g + 1)
                for j in range(GROUP):
                    last = dve.bn_aggr(x_mv[:, c % 2, j, :], x_st[:, j, :])
                last.then_inc(s_xmv, 1)

            def score_max(u, c):
                g = RING * u + c
                dve.wait_ge(s_sc, g + 1)
                if after(u, c, 2):
                    dve.wait_ge(s_prob, g - 1)
                dve.tensor_reduce(neg_max[:, c % 2], b_sc[:, 0:GROUP * K].rearrange("p (j k) -> p j k", k=K),
                                  AX_X, ALU.max, negate=True).then_inc(s_max, 1)

            def value_bias(u, c):
                g = RING * u + c
                dve.wait_ge(s_val_ps, g + 1)
                dve.wait_ge(s_wo, 2)
                if after(u, c, 2):
                    dve.wait_ge(s_att, g - 1)
                bias = bias_b[0:K, :].rearrange("p (a h) -> p a h", a=1).to_broadcast([K, GROUP, H])
                dve.tensor_tensor(vals[0:K, c % 2].rearrange("p (j h) -> p j h", h=H),
                                  b_val[0:K, :].rearrange("p (j h) -> p j h", h=H), bias, ALU.add).then_inc(s_val, 1)

            def residual(u, c):
                g, slot = RING * u + c, c % RING
                dve.wait_ge(s_prob, g + 1)
                dve.reciprocal(row_inv[:, :], row_sum[:, c % 2]).then_inc(s_inv, 1)
                dve.wait_ge(s_inv, g + 1)
                dve.wait_ge(s_att, g + 1)
                if after(u, c, 2):
                    dve.wait_ge(s_z, g - 1)
                for j in range(GROUP):
                    last = dve.scalar_tensor_tensor(x1[:, c % 2, j, :], b_att[:, j * H:(j + 1) * H],
                                                    row_inv[:, j:j + 1], x_sb[:, slot, j, :], ALU.mult, ALU.add)
                last.then_inc(s_x1, 1)
                dve.wait_ge(s_x1, g + 1)
                for j in range(GROUP):
                    last = dve.bn_stats(z_st[:, j, :], x1[:, c % 2, j, :])
                last.then_inc(s_zst, 1)
                wait_reg(s_zst, g + 1)
                for j in range(GROUP):
                    last = dve.bn_aggr(z_mv[:, c % 2, j, :], z_st[:, j, :])
                last.then_inc(s_zmv, 1)

            def squares(u, c, lo, hi):
                g = RING * u + c
                if lo == 0:
                    dve.wait_ge(s_xmv, g + 1)
                    dve.tensor_scalar(sq[:, c % 2, 0, :], x_mv[:, c % 2, :, 1], EPS, float(H),
                                      ALU.add, ALU.mult).then_inc(s_xsq, 1)
                if hi == 3:
                    dve.wait_ge(s_zmv, g - 2)
                    var = z_mv[:, (c + 1) % 2, :, 1]
                    dve.tensor_scalar(sq[:, c % 2, 1, :], var, 1.0 + EPS, EPS * EPS, ALU.mult, ALU.add)
                    dve.tensor_scalar(sq[:, c % 2, 2, :], var, EPS, None, ALU.add).then_inc(s_zsq, 1)

            def roots(u, c, lo, hi):
                t, h = RING * u + c, c % 2
                dve.wait_ge(s_root0, t + 1)
                y = root0[:, lo:hi, :]
                dve.tensor_tensor(root0_2[:, lo:hi, :], y, y, ALU.mult).then_inc(s_root02, 1)
                dve.wait_ge(s_root02, t + 1)
                if after(u, c, 3):
                    dve.wait_ge(s_rerr, t)
                dve.scalar_tensor_tensor(root_err[:, lo:hi, :], root0_2[:, lo:hi, :], -0.5, sq[:, h, lo:hi, :],
                                         ALU.mult, ALU.mult).then_inc(s_rerr, 1)
                dve.wait_ge(s_rerr, t + 1)
                if after(u, c, 5):
                    dve.wait_ge(s_z, t - 4)
                dve.scalar_tensor_tensor(root[:, h, lo:hi, :], root_err[:, lo:hi, :], 1.5, y,
                                         ALU.add, ALU.mult).then_inc(s_root, 1)

            def x_scalars(u, c):
                g = RING * u + c
                dve.wait_ge(s_root, g + 1)
                dve.scalar_tensor_tensor(x_bias[:, c % 2], x_mv[:, c % 2, :, 0], -1.0, root[:, c % 2, 0, :],
                                         ALU.mult, ALU.mult).then_inc(s_xb, 1)

            def z_scalars(u, c):
                g, slot, h = RING * u + c, c % RING, (c + 1) % 2
                mine = rows[:, GROUP * slot:GROUP * slot + GROUP, :]
                dve.wait_ge(s_root, g + 4)
                dve.scalar_tensor_tensor(z_bias[:, c % 2], z_mv[:, c % 2, :, 0], -1.0, root[:, h, 1, :],
                                         ALU.mult, ALU.mult).then_inc(s_zb, 1)
                dve.tensor_tensor(z_len[:, :], sq[:, h, 1, :], root[:, h, 1, :], ALU.mult).then_inc(s_zlen, 1)
                dve.tensor_scalar(z_t[:, :], root[:, h, 2, :], tanh_g[:, 1:2], 1.0, ALU.mult, ALU.add).then_inc(s_zt, 1)
                if after(u, c, RING):
                    dve.wait_ge(sent[slot], 16 * GROUP * (u + c // RING))
                dve.tensor_copy(mine[:, :, MEAN], z_mv[:, c % 2, :, 0])
                dve.wait_ge(s_zt, g + 1)
                dve.tensor_tensor(mine[:, :, Z_SCALE], z_t[:, :], z_len[:, :], ALU.mult).then_inc(s_zsc, 1)

            rev = expert_rev[:, :].rearrange("p (a e) -> p a e", a=1).to_broadcast([P, PT, E])

            def over_experts(v):
                return v.rearrange("p (t a) -> p t a", a=1).to_broadcast([P, PT, E])

            def choose(u, c):
                p = 2 * u + c // 2
                dve.wait_ge(s_lg, 2 * p + 2)
                dve.tensor_copy(lg[:, :, :], lg_ps).then_inc(s_lg_sb, 1)
                dve.wait_ge(s_lg_sb, p + 1)
                if after(u, c, 2):
                    dve.wait_ge(s_elg, p)
                dve.tensor_reduce(lg_max[:, :], lg[:, :, :], AX_X, ALU.max).then_inc(s_lmax, 1)
                dve.wait_ge(s_lmax, p + 1)
                dve.tensor_tensor(hit[:, :, :], lg[:, :, :], over_experts(lg_max[:, :]), ALU.is_equal).then_inc(s_hit, 1)
                dve.wait_ge(s_hit, p + 1)
                dve.tensor_tensor(hit_rev[:, :, :], hit[:, :, :], rev, ALU.mult).then_inc(s_rev, 1)
                dve.wait_ge(s_rev, p + 1)
                dve.tensor_reduce(best_rev[:, :], hit_rev[:, :, :], AX_X, ALU.max).then_inc(s_best, 1)
                dve.wait_ge(s_best, p + 1)
                if after(u, c, 2):
                    dve.wait_ge(s_rank, p)
                dve.tensor_tensor(onehot[:, 0:PT, :], rev, over_experts(best_rev[:, :]), ALU.is_equal).then_inc(s_hot, 1)

            def positions(u, c):
                p = 2 * u + c // 2
                dve.wait_ge(s_rank, p + 1)
                dve.wait_ge(s_free, p + 1)
                free = first_free[:, :].rearrange("p (a e) -> p a e", a=1).to_broadcast([P, PT, E])
                dve.tensor_tensor(place[:, :, :], rank_ps[:, 0:PT, :], free, ALU.add).then_inc(s_place, 1)
                dve.wait_ge(s_place, p + 1)
                dve.tensor_tensor(first_free[:, :], rank_ps[:, PT, :], first_free[:, :], ALU.add).then_inc(s_free, 1)
                dve.wait_ge(s_hot, p + 1)
                dve.tensor_tensor(place_hit[:, :, :], place[:, :, :], onehot[:, 0:PT, :], ALU.mult).then_inc(s_phit, 1)
                dve.wait_ge(s_elg, p + 1)
                dve.tensor_scalar(exp_lg1[:, :], exp_lg[:, :], 1.0, None, ALU.add).then_inc(s_elg1, 1)
                dve.wait_ge(s_phit, p + 1)
                dve.tensor_reduce(pos_f[:, :], place_hit[:, :, :], AX_X, ALU.add).then_inc(s_posf, 1)
                dve.wait_ge(s_elg1, p + 1)
                half = PT * ((c // 2) % 2)
                dve.reciprocal(rows[:, half:half + PT, SCORE], exp_lg1[:, :]).then_inc(s_score, 1)
                dve.wait_ge(s_posf, p + 1)
                if after(u, c, RING):
                    for s in (c % RING, (c + 1) % RING):
                        dve.wait_ge(sent[s], 16 * GROUP * (u + c // RING))
                dve.tensor_copy(pos[:, (c // 2) % 2, :], pos_f[:, :]).then_inc(s_pos, 1)

            dve.wait_ge(s_const, CONSTS)

            def step(u, c):
                routed = c % 2 == 0 and live(u, c - 6, GROUPS)
                if routed:
                    choose(u, c - 6)
                if live(u, c - 3, GROUPS):
                    residual(u, c - 3)
                if live(u, c, GROUPS):
                    x_stats(u, c)
                lo, hi = (0 if live(u, c, GROUPS) else 1), (3 if live(u, c - 3, GROUPS) else 1)
                if lo < hi:
                    squares(u, c, lo, hi)
                if lo < hi:
                    roots(u, c, lo, hi)
                if live(u, c, GROUPS):
                    x_scalars(u, c)
                if live(u, c - 3, GROUPS):
                    z_scalars(u, c - 3)
                if live(u, c - 1, GROUPS):
                    score_max(u, c - 1)
                    value_bias(u, c - 1)
                if routed:
                    positions(u, c - 6)

            run_steps(dve, step, GROUPS + 4, 2 * RING, GROUPS)

            made = [0]

            def link(ins):
                made[0] += 1
                ins.then_inc(s_tab, 1)
                dve.wait_ge(s_tab, made[0])

            NT = TOKENS // P
            dve.wait_ge(s_free, PAIRS + 1)
            link(dve.tensor_copy(fill_row[:, :], first_free[:, :]))
            link(dve.tensor_tensor(counts[:, :], first_free[:, :], region_at[:, :], ALU.subtract))
            link(dve.tensor_tensor(over[:, :, :], counts[:, :].rearrange("p (e a) -> p e a", a=1).to_broadcast([P, E, NT]),
                                   steps128[:, :].rearrange("p (a n) -> p a n", a=1).to_broadcast([P, E, NT]), ALU.is_gt))
            link(dve.tensor_reduce(n_tiles[:, :], over[:, :, :], AX_X, ALU.add))
            link(dve.tensor_copy(cum[:, 0, :], n_tiles[:, :]))
            for i, d in enumerate((1, 2, 4)):
                link(dve.tensor_copy(cum[:, i + 1, 0:d], cum[:, i, 0:d]))
                link(dve.tensor_tensor(cum[:, i + 1, d:E], cum[:, i, d:E], cum[:, i, 0:E - d], ALU.add))
            cums = cum[:, 3, :].rearrange("p (a e) -> p a e", a=1).to_broadcast([P, TILES, E])
            link(dve.tensor_tensor(past[:, :, :], tile_no[:, :].rearrange("p (t a) -> p t a", a=1).to_broadcast([P, TILES, E]),
                                   cums, ALU.is_ge))
            link(dve.tensor_reduce(tile_e[:, :], past[:, :, :], AX_X, ALU.add))
            link(dve.tensor_tensor(past_cum[:, :, :], past[:, :, :], cums, ALU.mult))
            link(dve.tensor_reduce(tile_c[:, :], past_cum[:, :, :], AX_X, ALU.max))
            link(dve.tensor_tensor(tile_a[:, :], tile_no[:, :], tile_c[:, :], ALU.subtract))
            link(dve.tensor_scalar(tile_b[:, :], tile_e[:, :], float(REGION), None, ALU.mult))
            link(dve.scalar_tensor_tensor(tile_c[:, :], tile_a[:, :], float(P), tile_b[:, :], ALU.mult, ALU.add))
            link(dve.tensor_scalar(tile_row[:, :], tile_c[:, :], float(E * REGION), None, ALU.min))
            link(dve.tensor_scalar(tile_expert[:, :], tile_e[:, :], float(E - 1), None, ALU.min))
            dve.engine_nop().then_inc(s_table, 1)

            def hiddenT(u, c):
                k = RING * u + c
                dve.wait_ge(s_hT_ps, k + 1)
                if after(u, c, 2):
                    dve.wait_ge(s_dn, k - 1)
                dve.tensor_copy(hidT_r[:, c % 2], b_hT[:, 0:I]).then_inc(s_hT, 1)

            def hidden(u, c):
                k, slot = RING * u + c, c % RING
                dve.wait_ge(s_ar, k + 1)
                if after(u, c, 2):
                    dve.wait_ge(s_hT_ps, k - 1)
                dve.scalar_tensor_tensor(hid_r[:, c % 2], b_gur[c % 2][:, I:2 * I], srow[:, slot, SCORE:SCORE + 1],
                                         act_r[:, c % 2], ALU.mult, ALU.mult).then_inc(s_hr, 1)
                dve.wait_ge(s_as, k + 1)
                if after(u, c, 2):
                    dve.wait_ge(s_dn, k - 1)
                dve.tensor_tensor(hid_s[:, c % 2], b_gus[c % 2][:, I:2 * I], act_s[:, c % 2], ALU.mult).then_inc(s_hs, 1)

            def result(u, c):
                k, slot = RING * u + c, c % RING
                dve.wait_ge(s_dn, k + 1)
                dve.wait_ge(s_base, k + 1)
                if after(u, c, RING):
                    dve.wait_ge(stored[slot], 16 * (u + c // RING))
                dve.tensor_tensor(res[:, slot, :], b_dn[c % 2][:, 0:H], base[:, slot, :], ALU.add).then_inc(s_res, 1)

            def step2(u, c):
                if live(u, c - 2, TILES):
                    hiddenT(u, c - 2)
                if live(u, c - 1, TILES):
                    hidden(u, c - 1)
                if live(u, c - 2, TILES):
                    result(u, c - 2)

            run_steps(dve, step2, TILES + 1, 2 * RING, TILES)

        @block.tensor
        def _(pe):
            pe.wait_ge(s_const, CONSTS)
            pe.wait_ge(s_small, 16 * 7)
            pe.transpose(b_sc[:, 0:H], w_out_sb[:, :], ident[:, :]).then_inc(s_woT, 1)
            pe.wait_ge(s_wo, 2)

            def transposes(u, c):
                g, slot = RING * u + c, c % RING
                pe.wait_ge(s_n1, g + 1)
                if after(u, c, 1):
                    pe.wait_ge(s_n1T, g)
                for j in range(GROUP):
                    last = pe.transpose(b_n1T[:, j * P:(j + 1) * P], n1[:, c % 2, j, :], ident[:, :])
                last.then_inc(s_n1T_ps, 1)
                pe.wait_ge(c_in[slot], 16 * (u + c // RING + 1))
                if after(u, c, 1):
                    pe.wait_ge(s_ctxT, g)
                for j in range(GROUP):
                    last = pe.transpose(b_ctxT[:, j * K:(j + 1) * K], ctx_sb[0:K, slot, j, :], ident[0:K, 0:K])
                last.then_inc(s_ctxT_ps, 1)

            def z_transposes(u, c):
                g, slot = RING * u + c, c % RING
                pe.wait_ge(s_z, g + 1)
                if after(u, c, 1):
                    pe.wait_ge(s_xfT, g)
                for j in range(GROUP):
                    last = pe.transpose(b_zT[:, j * P:(j + 1) * P], rows[:, GROUP * slot + j, 0:H], ident[:, :])
                last.then_inc(s_zT_ps, 1)

            def scores(u, c):
                g = RING * u + c
                pe.wait_ge(s_n1T, g + 1)
                pe.wait_ge(s_ctxT, g + 1)
                if after(u, c, 1):
                    pe.wait_ge(s_prob, g)
                for j in range(GROUP):
                    last = pe.matmul(b_sc[:, j * K:(j + 1) * K], n1T[:, j * P:(j + 1) * P],
                                     ctxT[:, j * K:(j + 1) * K], start=True, stop=True)
                last.then_inc(s_sc, 1)
                if after(u, c, 1):
                    pe.wait_ge(s_val, g)
                for j in range(GROUP):
                    last = pe.matmul(b_val[0:K, j * H:(j + 1) * H], ctxT[:, j * K:(j + 1) * K], w_out_t[:, :],
                                     start=True, stop=True)
                last.then_inc(s_val_ps, 1)

            def logits(u, c):
                g = RING * u + c
                p = 2 * u + c // 2
                pe.wait_ge(s_xfT, g + 1)
                if after(u, c, 2):
                    if c % 2 == 0:
                        pe.wait_ge(s_lg_sb, p)
                    else:
                        pe.wait_ge(s_free, p + 1)
                for j in range(GROUP):
                    last = pe.matmul(lg_ps[:, (c % 2) * GROUP + j, :], xfT[:, j * P:(j + 1) * P], router[:, :],
                                     start=True, stop=True)
                last.then_inc(s_lg, 1)

            def probs_transposes(u, c):
                g = RING * u + c
                pe.wait_ge(s_prob, g + 1)
                if after(u, c, 1):
                    pe.wait_ge(s_pT, g)
                for j in range(GROUP):
                    last = pe.transpose(b_pT[0:K, j * P:(j + 1) * P], probs[:, j, :], ident[:, :])
                last.then_inc(s_pT_ps, 1)

            def attend(u, c):
                g = RING * u + c
                pe.wait_ge(s_pT, g + 1)
                pe.wait_ge(s_val, g + 1)
                if after(u, c, 1):
                    pe.wait_ge(s_x1, g)
                for j in range(GROUP):
                    last = pe.matmul(b_att[:, j * H:(j + 1) * H], probsT[0:K, j * P:(j + 1) * P],
                                     vals[0:K, c % 2, j * H:(j + 1) * H], start=True, stop=True)
                last.then_inc(s_att, 1)

            def ranks(u, c):
                p = 2 * u + c // 2
                pe.wait_ge(s_hot, p + 1)
                pe.wait_ge(s_free, p + 1)
                pe.matmul(rank_ps, before[:, :], onehot[:, :, :], start=True, stop=False)
                for t in range(PT):
                    later = PT - t
                    last = pe.matmul(rank_ps[:, t + 1:PT + 1, :], ones[:, :],
                                     onehot[:, t:t + 1, :].to_broadcast([P, later, E]),
                                     start=False, stop=(t == PT - 1))
                last.then_inc(s_rank, 1)

            def step(u, c):
                if live(u, c - 1, GROUPS):
                    transposes(u, c - 1)
                if live(u, c - 2, GROUPS):
                    probs_transposes(u, c - 2)
                if live(u, c - 4, GROUPS):
                    z_transposes(u, c - 4)
                if live(u, c - 1, GROUPS):
                    scores(u, c - 1)
                if live(u, c - 2, GROUPS):
                    attend(u, c - 2)
                if live(u, c - 4, GROUPS):
                    logits(u, c - 4)
                if c % 2 == 0 and live(u, c - 6, GROUPS):
                    ranks(u, c - 6)

            run_steps(pe, step, GROUPS + 4, 2 * RING, GROUPS)

            pe.wait_ge(s_table, 1)
            pe.wait_ge(s_big, 16 * 6)
            pe.wait_ge(s_down, 1)
            pe.wait_ge(s_free, PAIRS + 1)

            def z_transpose(u, c):
                k, slot = RING * u + c, c % RING
                pe.wait_ge(r_in[slot], 16 * (u + c // RING + 1))
                if after(u, c, 1):
                    pe.wait_ge(s_xfT2, k)
                pe.transpose(b_zT2[:, 0:P], srow[:, slot, 0:H], ident[:, :]).then_inc(s_zT2_ps, 1)

            def gate_and_up(u, c):
                k = RING * u + c
                expert = pe.value_load(tile_expert[0:1, bass.ds(k, 1)], min_val=0, max_val=E - 1)
                pe.wait_ge(s_xfT2, k + 1)
                if after(u, c, 2):
                    pe.wait_ge(s_hr, k - 1)
                xf = xfT2[:, c % 2]
                pe.matmul(b_gur[c % 2][:, :], xf, gate_up[:, bass.ds(expert, 1), :].rearrange("p a n -> p (a n)"),
                          start=True, stop=True).then_inc(s_gur, 1)
                if after(u, c, 2):
                    pe.wait_ge(s_hs, k - 1)
                for n in range(2 * CHUNKS):
                    last = pe.matmul(b_gus[c % 2][:, n * P:(n + 1) * P], sh_gu[:, n * P:(n + 1) * P], xf,
                                     start=True, stop=True)
                last.then_inc(s_gus, 1)

            def hidden_transposes(u, c):
                k = RING * u + c
                pe.wait_ge(s_hr, k + 1)
                if after(u, c, 1):
                    pe.wait_ge(s_hT, k)
                for n in range(CHUNKS):
                    last = pe.transpose(b_hT[:, n * P:(n + 1) * P], hid_r[:, c % 2, n * P:(n + 1) * P], ident[:, :])
                last.then_inc(s_hT_ps, 1)

            def down_products(u, c):
                k = RING * u + c
                expert = pe.value_load(tile_expert[0:1, bass.ds(k, 1)], min_val=0, max_val=E - 1)
                pe.wait_ge(s_hs, k + 1)
                if after(u, c, 2):
                    pe.wait_ge(s_res, k - 1)
                for n in range(CHUNKS):
                    pe.matmul(b_dn[c % 2][:, 0:H], hid_s[:, c % 2, n * P:(n + 1) * P], down[:, E, n, :],
                              start=(n == 0), stop=False)
                pe.wait_ge(s_hT, k + 1)
                for n in range(CHUNKS):
                    last = pe.matmul(b_dn[c % 2][:, 0:H], hidT_r[:, c % 2, n * P:(n + 1) * P],
                                     down[:, bass.ds(expert, 1), n, :].rearrange("p a n -> p (a n)"),
                                     start=False, stop=(n == CHUNKS - 1))
                last.then_inc(s_dn, 1)

            def step2(u, c):
                if live(u, c - 2, TILES):
                    hidden_transposes(u, c - 2)
                if live(u, c - 1, TILES):
                    gate_and_up(u, c - 1)
                if live(u, c, TILES):
                    z_transpose(u, c)
                if live(u, c - 2, TILES):
                    down_products(u, c - 2)

            run_steps(pe, step2, TILES + 1, RING, TILES)


_INS = ["x", "ctx_1024", "g_xattn", "g_ffn", "L0_xattn_W_out", "L0_xattn_b_out", "L0_ffn_ln_w", "L0_ffn_ln_b",
        "L0_ffn_router_w", "L0_ffn_gate_w", "L0_ffn_up_w", "L0_ffn_down_w", "L0_ffn_sh_gate", "L0_ffn_sh_up",
        "L0_ffn_sh_down"]


def kernel(**inputs):
    import numpy as np
    import concourse.bacc as bacc
    from concourse import mybir as mb
    from concourse.bass_utils import run_bass_kernel_spmd

    nc = bacc.Bacc("TRN2", target_bir_lowering=False, num_devices=1)
    arrays, args = {}, []
    for name in _INS:
        a = np.ascontiguousarray(inputs[name])
        arrays[f"in_{name}"] = a
        args.append(nc.dram_tensor(f"in_{name}", a.shape, mb.dt.from_np(a.dtype), kind="ExternalInput").ap())
    shape = tuple(inputs["x"].shape)
    args.append(nc.dram_tensor("out_0", shape, mb.dt.float32, kind="ExternalOutput").ap())
    flamingo_kernel(nc, *args)
    r = run_bass_kernel_spmd(nc, [arrays], core_ids=[0])
    return r.results[0]["out_0"]
```

```python
from contextlib import ExitStack

import concourse.bass as bass
from concourse import mybir

ALU = mybir.AluOpType
ACT = mybir.ActivationFunctionType
F32 = mybir.dt.float32
BF16 = mybir.dt.bfloat16
F32R = mybir.dt.float32r
I32 = mybir.dt.int32
AX_X = mybir.AxisListType.X

P = 128
EPS = 1e-5
GROUP = 4
RING = 4


def flamingo_kernel(nc, x, ctx_in, g_xattn, g_ffn, w_out, b_out, ln_w, ln_b, router_w,
                    gate_w, up_w, down_w, sh_gate, sh_up, sh_down, out):
    B, S, H = x.shape
    K = ctx_in.shape[1]
    E, _, I = gate_w.shape
    assert S == P and H == P and K < P and B % (GROUP * RING) == 0 and I == 2 * P
    GROUPS = B // GROUP
    PAIRS = GROUPS // 2
    PT = 2 * GROUP
    TOKENS = B * S
    CHUNKS = I // P
    REGION = TOKENS + P
    TILES_USED = TOKENS // P + E - 1
    TILE_PAIRS = (TILES_USED + 1) // 2
    TILES = 2 * TILE_PAIRS
    BODY = 2 * RING
    assert TILE_PAIRS % RING == 0 and E <= 8 and BODY <= 8
    Z_ROOT, LN_ROOT, Z_BIAS, EXP_LG, TOKEN = H, H + 1, H + 2, H + 3, H + 4
    ROW = H + 5
    NO_TOKEN = 1 << 20
    WEIGHTS = 6
    SMALL = 16 * 5
    CONSTS = 10

    scratch = nc.dram_tensor("sorted_rows", [E * REGION + P, ROW], F32).ap()
    out_rows = out.rearrange("b s h -> (b s) h")
    x_v = x.rearrange("b s h -> s b h")
    ctx_v = ctx_in.rearrange("b k h -> k b h")

    with ExitStack() as stack:
        def sb(name, shape, dt=F32):
            return stack.enter_context(nc.sbuf_tensor(name, shape, dt))

        def sem(name):
            return stack.enter_context(nc.semaphore(name))

        banks = [stack.enter_context(nc.psum_tensor(f"bank{i}", [P, 512], F32)) for i in range(8)]

        ident = sb("ident", [P, P])
        ones = sb("ones", [P, P], BF16)
        before = sb("before", [P, P], BF16)
        expert_rev = sb("expert_rev", [P, E])
        gates = sb("gates", [P, 2])
        tanh_g = sb("tanh_g", [P, 2])
        w_out_sb = sb("w_out_sb", [P, H])
        w_out_t = sb("w_out_t", [P, H])
        bias_raw = sb("bias_raw", [P, H])
        lnw = sb("lnw", [P, 1])
        lnb = sb("lnb", [P, 1])
        router = sb("router", [P, E])
        router_w_ln = sb("router_w_ln", [P, E])
        router_x4 = sb("router_x4", [P, GROUP, E])
        lnb_b = sb("lnb_b", [P, P])
        gate_up = sb("gate_up", [P, E + 1, 2 * I])
        gate_up_hi = sb("gate_up_hi", [P, E + 1, 2 * I], F32R)
        gate_up_lo = sb("gate_up_lo", [P, E + 1, 2 * I], F32R)
        down_raw = sb("down_raw", [P, E + 1, CHUNKS, H])
        down = sb("down", [P, E + 1, CHUNKS, H])

        x_sb = sb("x_sb", [P, RING, GROUP, H])
        ctx_sb = sb("ctx_sb", [P, RING, GROUP, H])
        x_st = sb("x_st", [P, GROUP, 6])
        x_mv = sb("x_mv", [P, 2, GROUP, 2])
        z_mv = sb("z_mv", [P, 2, GROUP, 2])
        sq = sb("sq", [P, 2, 3, GROUP])
        ln_sq = sb("ln_sq", [P, 3, GROUP])
        root0 = sb("root0", [P, 3, GROUP])
        root0_2 = sb("root0_2", [P, 3, GROUP])
        root_err = sb("root_err", [P, 3, GROUP])
        root = sb("root", [P, 2, 4, GROUP])
        x_bias = sb("x_bias", [P, 2, GROUP])
        n1 = sb("n1", [P, 2, GROUP, H])
        n1T = sb("n1T", [P, GROUP * P])
        ctxT = sb("ctxT", [P, GROUP * K])
        neg_max = sb("neg_max", [P, 2, GROUP])
        probs = sb("probs", [P, 2, GROUP, K + 1])
        row_inv = sb("row_inv", [P, GROUP])
        probsT = sb("probsT", [P, GROUP * P])
        vals = sb("vals", [P, 2, GROUP * H])
        x1 = sb("x1", [P, 2, GROUP, H])
        z_st = sb("z_st", [P, GROUP, 6])
        rows = sb("rows", [P, RING * GROUP, ROW])
        rows_i = rows[:, :, :].bitcast(I32)
        zT = sb("zT", [P, GROUP * P])
        lg_max = sb("lg_max", [P, PT])
        hit = sb("hit", [P, PT, E])
        hit_rev = sb("hit_rev", [P, PT, E])
        best_rev = sb("best_rev", [P, PT])
        onehot = sb("onehot", [P, PT + 1, E], BF16)
        place = sb("place", [P, PT, E])
        place_hit = sb("place_hit", [P, PT, E])
        pos_f = sb("pos_f", [P, PT])
        pos = sb("pos", [P, 2, PT], I32)
        first_free = sb("first_free", [P, E])

        region_at = sb("region_at", [P, E])
        counts = sb("counts", [P, E])
        steps128 = sb("steps128", [P, TOKENS // P])
        over = sb("over", [P, E, TOKENS // P])
        n_tiles = sb("n_tiles", [P, E])
        cum = sb("cum", [P, 4, E])
        tile_no = sb("tile_no", [P, TILES])
        past = sb("past", [P, TILES, E])
        past_cum = sb("past_cum", [P, TILES, E])
        tile_e = sb("tile_e", [P, TILES])
        tile_c = sb("tile_c", [P, TILES])
        tile_a = sb("tile_a", [P, TILES])
        tile_b = sb("tile_b", [P, TILES])
        tile_row = sb("tile_row", [P, TILES], I32)
        bit_place = sb("bit_place", [P, BODY])
        placed = sb("placed", [P, TILES // BODY, BODY])
        body_experts_f = sb("body_experts_f", [P, TILES // BODY])
        body_experts = sb("body_experts", [P, TILES // BODY], I32)
        fill_row = sb("fill_row", [P, E], I32)
        filling = sb("filling", [P, ROW])
        filling_i = filling[:, :].bitcast(I32)

        srow = sb("srow", [P, RING, 2, ROW])
        srow_i = srow[:, :, :, :].bitcast(I32)
        token = sb("token", [P, RING, 2], I32)
        base = sb("base", [P, RING, 2, H])
        exp_lg1 = sb("exp_lg1", [P, 2])
        z_len = sb("z_len", [P, 2])
        ln_factor = sb("ln_factor", [P, 2])
        score = sb("score", [P, RING, 2])
        z_scale = sb("z_scale", [P, RING, 2])
        mean = sb("mean", [P, RING, 2])
        xfT2 = sb("xfT2", [P, 2, 2 * P])
        xf_hi = sb("xf_hi", [P, 2, 2 * P], F32R)
        xf_lo = sb("xf_lo", [P, 2, 2 * P], F32R)
        act_r = sb("act_r", [P, 2, I])
        act_s = sb("act_s", [P, CHUNKS, 2 * P])
        hid_r = sb("hid_r", [P, 2, I])
        hid_s = sb("hid_s", [P, 2, CHUNKS, 2 * P])
        hidT_r = sb("hidT_r", [P, 2, 2, I])
        res = sb("res", [P, RING, 2, H])

        s_const = sem("s_const")
        s_const0 = sem("s_const0")
        s_small = sem("s_small")
        s_big = sem("s_big")
        s_tanh = sem("s_tanh")
        s_woT = sem("s_woT")
        s_wo = sem("s_wo")
        s_gu_hi, s_gu_lo = sem("s_gu_hi"), sem("s_gu_lo")
        s_down = sem("s_down")
        x_in = [sem(f"x_in{i}") for i in range(RING)]
        c_in = [sem(f"c_in{i}") for i in range(RING)]
        s_xst, s_xmv, s_xsq = sem("s_xst"), sem("s_xmv"), sem("s_xsq")
        s_xb = sem("s_xb")
        s_lnsq, s_root0, s_root02, s_rerr, s_root = sem("s_lnsq"), sem("s_root0"), sem("s_root02"), sem("s_rerr"), sem("s_root")
        s_n1 = sem("s_n1")
        s_n1T_ps, s_ctxT_ps, s_n1T, s_ctxT = sem("s_n1T_ps"), sem("s_ctxT_ps"), sem("s_n1T"), sem("s_ctxT")
        s_sc, s_val_ps, s_val = sem("s_sc"), sem("s_val_ps"), sem("s_val")
        s_max, s_prob = sem("s_max"), sem("s_prob")
        s_pT_ps, s_pT, s_att = sem("s_pT_ps"), sem("s_pT"), sem("s_att")
        s_inv, s_x1, s_zst, s_zmv = sem("s_inv"), sem("s_x1"), sem("s_zst"), sem("s_zmv")
        s_zsq, s_zb, s_zroot = sem("s_zsq"), sem("s_zb"), sem("s_zroot")
        s_z, s_zT_ps, s_zT, s_lg = sem("s_z"), sem("s_zT_ps"), sem("s_zT"), sem("s_lg")
        s_router = sem("s_router")
        s_lmax, s_hit, s_rev, s_best = sem("s_lmax"), sem("s_hit"), sem("s_rev"), sem("s_best")
        s_hot, s_rank, s_place, s_phit = sem("s_hot"), sem("s_rank"), sem("s_place"), sem("s_phit")
        s_free, s_posf, s_pos = sem("s_free"), sem("s_posf"), sem("s_pos")
        s_elg, s_token = sem("s_elg"), sem("s_token")
        s_gates = sem("s_gates")
        sent = [[sem(f"sent{i}_{j}") for j in range(GROUP)] for i in range(RING)]
        s_tab = sem("s_tab")
        s_table = sem("s_table")
        s_fill_row = sem("s_fill_row")
        s_fill = sem("s_fill")
        r_in = [sem(f"r_in{i}") for i in range(RING)]
        s_base = sem("s_base")
        s_part, s_score, s_scalars = sem("s_part"), sem("s_score"), sem("s_scalars")
        s_zT2_ps, s_xfT2, s_xf_lo = sem("s_zT2_ps"), sem("s_xfT2"), sem("s_xf_lo")
        s_gur, s_gus, s_ar, s_as = sem("s_gur"), sem("s_gus"), sem("s_ar"), sem("s_as")
        s_hr, s_hs, s_hT_ps, s_hT = sem("s_hr"), sem("s_hs"), sem("s_hT_ps"), sem("s_hT")
        s_dn, s_res = sem("s_dn"), sem("s_res")
        stored = [sem(f"stored{i}") for i in range(RING)]

        b_n1T, b_ctxT, b_sc, b_val, b_pT, b_att, b_zT, b_lg = banks
        lg_ps = b_lg[:, 0:PT * E].rearrange("p (t e) -> p t e", e=E)
        rank_ps = b_lg[:, 128:128 + (PT + 1) * E].rearrange("p (t e) -> p t e", e=E)
        b_zT2, b_hT, b_dn = banks[0], banks[1], banks[6]
        b_gur, b_gus = banks[2:4], banks[4:6]
        gus_v = [b[:, :].rearrange("p (m t) -> p m t", m=CHUNKS) for b in b_gus]

        def after(u, c, least):
            return not isinstance(u, int) or RING * u + c >= least

        def run_steps(eng, step, last, first_looped, end_looped):
            for t in range(first_looped):
                step(0, t)
            with eng.Fori(first_looped // RING, end_looped // RING) as u:
                for c in range(RING):
                    step(u, c)
            for t in range(end_looped, last + 1):
                step(0, t)

        def chosen(u, c):
            return c % 2 == 1 and live(u, c - 5, GROUPS)

        def placed_pair(u, c):
            if isinstance(u, int) and c == GROUPS + 3:
                return c - 5
            return c - 6 if c % 2 == 0 and live(u, c - 6, GROUPS) else None

        def live(u, c, count):
            return not isinstance(u, int) or 0 <= RING * u + c < count

        def tiles_of(u, c):
            return TILES_USED - 2 * c if isinstance(u, int) and c == TILE_PAIRS - 1 else 2

        block = stack.enter_context(nc.Block())

        @block.sync
        def _(sp):
            def load_group(u, c):
                g, slot = RING * u + c, c % RING
                if after(u, c, RING):
                    sp.wait_ge(s_x1, g - RING + 1)
                sp.dma_start(x_sb[:, slot], x_v[:, bass.ds(g * GROUP, GROUP), :]).then_inc(x_in[slot], 16)
                if after(u, c, RING):
                    sp.wait_ge(s_ctxT_ps, g - RING + 1)
                sp.dma_start(ctx_sb[0:K, slot], ctx_v[:, bass.ds(g * GROUP, GROUP), :]).then_inc(c_in[slot], 16)

            sp.dma_start(gates[:, 0:1], g_xattn.rearrange("(a h) -> a h", a=1).to_broadcast([P, 1])).then_inc(s_gates, 16)
            load_group(0, 0)
            sp.dma_start(w_out_sb[:, :], w_out).then_inc(s_small, 16)
            load_group(0, 1)
            sp.dma_start(bias_raw[:, :], b_out.rearrange("(a h) -> a h", a=1).to_broadcast([P, H])).then_inc(s_small, 16)
            sp.dma_start(lnw[:, :], ln_w.rearrange("(h a) -> h a", a=1)).then_inc(s_small, 16)
            sp.dma_start(lnb[:, :], ln_b.rearrange("(h a) -> h a", a=1)).then_inc(s_small, 16)
            sp.dma_start(router[:, :], router_w).then_inc(s_small, 16)
            for c in range(2, RING):
                load_group(0, c)
            sp.wait_ge(s_const, CONSTS)
            sp.dma_start(scratch[E * REGION:E * REGION + P, :], filling[:, :]).then_inc(s_fill, 16)
            sp.dma_start(down_raw[:, 0:E], down_w.rearrange("e (c p) h -> p e c h", p=P)).then_inc(s_big, 16)
            sp.dma_start(down_raw[:, E], sh_down.rearrange("(c p) h -> p c h", p=P)).then_inc(s_big, 16)
            sp.dma_start(gate_up[:, 0:E, 0:I], gate_w.rearrange("e h i -> h e i")).then_inc(s_big, 16)
            sp.dma_start(gate_up[:, 0:E, I:2 * I], up_w.rearrange("e h i -> h e i")).then_inc(s_big, 16)
            sp.dma_start(gate_up[:, E, 0:I], sh_gate).then_inc(s_big, 16)
            sp.dma_start(gate_up[:, E, I:2 * I], sh_up).then_inc(s_big, 16)
            with sp.Fori(1, GROUPS // RING) as u:
                for c in range(RING):
                    load_group(u, c)

            sp.wait_ge(s_fill_row, 1)
            for e in range(E // 2):
                at = sp.value_load(fill_row[0:1, e:e + 1], min_val=0, max_val=E * REGION)
                sp.dma_start(scratch[bass.ds(at, P), :], filling[:, :]).then_inc(s_fill, 16)
            sp.wait_ge(s_table, 1)
            first_rows = [sp.value_load(tile_row[0:1, k:k + 1], min_val=0, max_val=E * REGION) for k in range(4)]
            sp.wait_ge(s_fill, 16 * (E + 1))
            for slot in range(RING):
                for j in range(GROUP):
                    sp.wait_ge(sent[slot][j], 16 * (GROUPS // RING))

            def load_pair(u, c):
                n, slot = RING * u + c, c % RING
                sp.wait_ge(s_base, n - RING + 1)
                sp.wait_ge(s_zT2_ps, n - RING + 1)
                sp.wait_ge(s_scalars, n - RING + 1)
                sp.wait_ge(s_table, 1)
                for i in range(tiles_of(u, c)):
                    at = sp.value_load(tile_row[0:1, bass.ds(2 * n + i, 1)], min_val=0, max_val=E * REGION)
                    sp.dma_start(srow[:, slot, i], scratch[bass.ds(at, P), :]).then_inc(r_in[slot], 16)

            for k in range(2 * RING):
                if k < len(first_rows):
                    at = first_rows[k]
                else:
                    at = sp.value_load(tile_row[0:1, k:k + 1], min_val=0, max_val=E * REGION)
                sp.dma_start(srow[:, k // 2, k % 2], scratch[bass.ds(at, P), :]).then_inc(r_in[k // 2], 16)
            with sp.Fori(1, TILE_PAIRS // RING - 1) as u:
                for c in range(RING):
                    load_pair(u, c)
            for c in range(TILE_PAIRS - RING, TILE_PAIRS):
                load_pair(0, c)

        @block.gpsimd
        def _(pool):
            pool.memset(ident[:, :], 0.0).then_inc(s_const0, 1)
            pool.memset(before[:, :], 1.0).then_inc(s_const0, 1)
            pool.memset(ones[:, :], 1.0).then_inc(s_const, 1)
            pool.memset(onehot[:, :, :], 0.0).then_inc(s_const, 1)
            pool.memset(filling[:, :], 0.0).then_inc(s_const0, 1)
            pool.wait_ge(s_const0, 3)
            pool.affine_select(out=ident[:, :], in_=ident[:, :], compare_op=ALU.not_equal, fill=1.0,
                               base=0, pattern=[[-1, P]], channel_multiplier=1).then_inc(s_const, 1)
            pool.affine_select(out=before[:, :], in_=before[:, :], compare_op=ALU.is_gt, fill=0.0,
                               base=0, pattern=[[1, P]], channel_multiplier=-1).then_inc(s_const, 1)
            for i in range(BODY):
                last = pool.memset(bit_place[:, i:i + 1], float(8 ** i))
            last.then_inc(s_const, 1)
            pool.memset(filling[:, Z_ROOT:Z_ROOT + 1], 1.0)
            pool.memset(filling_i[:, TOKEN:TOKEN + 1], NO_TOKEN).then_inc(s_const, 1)
            pool.iota(expert_rev[:, :], pattern=[[-1, E]], base=E, channel_multiplier=0,
                      allow_small_or_imprecise_dtypes=True).then_inc(s_const, 1)
            pool.iota(first_free[:, :], pattern=[[REGION, E]], base=0, channel_multiplier=0,
                      allow_small_or_imprecise_dtypes=True).then_inc(s_free, 1)
            pool.iota(region_at[:, :], pattern=[[REGION, E]], base=0, channel_multiplier=0,
                      allow_small_or_imprecise_dtypes=True).then_inc(s_const, 1)
            pool.iota(steps128[:, :], pattern=[[P, TOKENS // P]], base=0, channel_multiplier=0,
                      allow_small_or_imprecise_dtypes=True).then_inc(s_const, 1)
            pool.iota(tile_no[:, :], pattern=[[1, TILES]], base=0, channel_multiplier=0,
                      allow_small_or_imprecise_dtypes=True).then_inc(s_const, 1)
            pool.iota(rows_i[:, :, TOKEN:TOKEN + 1], pattern=[[P, RING * GROUP], [0, 1]], base=0,
                      channel_multiplier=1).then_inc(s_token, RING)
            pool.wait_ge(s_const, CONSTS)

            def wait_reg(sem, count):
                if not isinstance(count, int):
                    count = pool.to_reg(count)
                    pool.wait_ge(s_const, CONSTS)
                pool.wait_ge(sem, count)

            def x_norm(u, c):
                g, slot = RING * u + c, c % RING
                wait_reg(s_xb, g + 1)
                if after(u, c, 2):
                    wait_reg(s_n1T_ps, g - 1)
                for j in range(GROUP):
                    last = pool.tensor_scalar(n1[:, c % 2, j, :], x_sb[:, slot, j, :], root[:, c % 2, 0, j:j + 1],
                                              x_bias[:, c % 2, j:j + 1], ALU.mult, ALU.add)
                last.then_inc(s_n1, 1)

            def scatter(u, c):
                g, slot = RING * u + c, c % RING
                p = 2 * u + c // 2
                wait_reg(s_pos, p + 1)
                wait_reg(s_elg, p + 1)
                wait_reg(s_zroot, g + 1)
                wait_reg(s_token, g + 1)
                for j in range(GROUP):
                    pool.indirect_dma_start(
                        out=scratch, out_offset=bass.IndirectOffsetOnAxis(
                            ap=pos[:, (c // 2) % 2, (c % 2) * GROUP + j:(c % 2) * GROUP + j + 1], axis=0),
                        in_=rows[:, GROUP * slot + j, :], in_offset=None).then_inc(sent[slot][j], 16)

            def next_tokens(u, c):
                g, slot = RING * u + c, c % RING
                for j in range(GROUP):
                    wait_reg(sent[slot][j], 16 * (u + c // RING + 1))
                mine = rows_i[:, GROUP * slot:GROUP * slot + GROUP, TOKEN]
                pool.tensor_scalar(mine, mine, RING * GROUP * P, None, ALU.add).then_inc(s_token, 1)

            def step(u, c):
                if live(u, c - 7, GROUPS):
                    scatter(u, c - 7)
                if live(u, c - 8, GROUPS - RING):
                    next_tokens(u, c - 8)
                if live(u, c, GROUPS):
                    x_norm(u, c)

            run_steps(pool, step, GROUPS + 6, 2 * RING, GROUPS)

            def base_of(u, c):
                n, slot = RING * u + c, c % RING
                wait_reg(s_scalars, n + 1)
                if after(u, c, RING):
                    wait_reg(s_res, n - RING + 1)
                    wait_reg(stored[slot], 32 * (u + c // RING))
                tiles = tiles_of(u, c)
                pool.tensor_copy(token[:, slot, 0:tiles], srow_i[:, slot, 0:tiles, TOKEN])
                for i in range(tiles):
                    last = pool.tensor_scalar(base[:, slot, i, :], srow[:, slot, i, 0:H], z_scale[:, slot, i:i + 1],
                                              mean[:, slot, i:i + 1], ALU.mult, ALU.add)
                last.then_inc(s_base, 1)

            def store(u, c):
                n, slot = RING * u + c, c % RING
                wait_reg(s_res, n + 1)
                wait_reg(s_base, n + 1)
                for i in range(tiles_of(u, c)):
                    pool.indirect_dma_start(
                        out=out_rows, out_offset=bass.IndirectOffsetOnAxis(ap=token[:, slot, i:i + 1], axis=0),
                        in_=res[:, slot, i, :], in_offset=None,
                        bounds_check=TOKENS - 1, oob_is_err=False).then_inc(stored[slot], 16)

            def step2(u, c):
                if live(u, c, TILE_PAIRS):
                    base_of(u, c)
                if live(u, c - 2, TILE_PAIRS):
                    store(u, c - 2)

            run_steps(pool, step2, TILE_PAIRS + 1, RING, TILE_PAIRS - RING)
            for slot in range(RING):
                unused = TILES - TILES_USED if slot == RING - 1 else 0
                pool.wait_ge(stored[slot], 32 * (TILE_PAIRS // RING) - 16 * unused)

        @block.scalar
        def _(act):
            act.dma_start(gates[:, 1:2], g_ffn.rearrange("(a h) -> a h", a=1).to_broadcast([P, 1])).then_inc(s_gates, 16)
            act.wait_ge(s_gates, 16 * 2)
            act.activation(tanh_g[:, :], gates[:, :], ACT.Tanh).then_inc(s_tanh, 1)
            act.preload_act_table_set("natural_log_exp_and_others")

            def prepare():
                act.wait_ge(s_tanh, 1)
                act.wait_ge(s_small, SMALL)
                at = slice(K // 32 * 32, K + 1)
                for h in range(2):
                    act.activation(vals[at, h, :].rearrange("p (j h) -> p j h", h=H),
                                   bias_raw[at, :].rearrange("p (a h) -> p a h", a=1).to_broadcast([K + 1 - K // 32 * 32, GROUP, H]),
                                   ACT.Copy, scale=tanh_g[at, 0:1]).then_inc(s_wo, 1)
                act.wait_ge(s_woT, 1)
                act.activation(w_out_t[:, :], b_sc[:, 0:H], ACT.Copy, scale=tanh_g[:, 0:1]).then_inc(s_wo, 1)
                act.activation(router_w_ln[:, :], router[:, :], ACT.Copy, scale=lnw[:, :]).then_inc(s_router, 1)
                act.activation(router_x4[:, :, :], router[:, :].rearrange("p (a e) -> p a e", a=1).to_broadcast([P, GROUP, E]),
                               ACT.Copy).then_inc(s_router, 1)
                act.activation(lnb_b[:, :], lnb[:, :].to_broadcast([P, P]), ACT.Copy).then_inc(s_router, 1)

            def copy_n1(u, c):
                g = RING * u + c
                act.wait_ge(s_n1T_ps, g + 1)
                if after(u, c, 1):
                    act.wait_ge(s_sc, g)
                act.activation(n1T[:, :], b_n1T[:, :], ACT.Copy).then_inc(s_n1T, 1)

            def copy_context(u, c):
                g = RING * u + c
                act.wait_ge(s_ctxT_ps, g + 1)
                if after(u, c, 1):
                    act.wait_ge(s_val_ps, g)
                act.activation(ctxT[:, :], b_ctxT[:, 0:GROUP * K], ACT.Copy).then_inc(s_ctxT, 1)

            def copy_z(u, c):
                g = RING * u + c
                act.wait_ge(s_zT_ps, g + 1)
                if after(u, c, 1):
                    act.wait_ge(s_lg, g)
                act.activation(zT[:, :], b_zT[:, :], ACT.Copy).then_inc(s_zT, 1)

            def copy_probs(u, c):
                g = RING * u + c
                act.wait_ge(s_pT_ps, g + 1)
                if after(u, c, 1):
                    act.wait_ge(s_att, g)
                act.activation(probsT[0:K + 1, :], b_pT[0:K + 1, :], ACT.Copy).then_inc(s_pT, 1)

            def copy_values(u, c):
                g = RING * u + c
                act.wait_ge(s_val_ps, g + 1)
                act.wait_ge(s_wo, 3)
                if after(u, c, 2):
                    act.wait_ge(s_att, g - 1)
                act.activation(vals[0:K, c % 2], b_val[0:K, :], ACT.Copy).then_inc(s_val, 1)

            def softmax_exp(u, c):
                g = RING * u + c
                act.wait_ge(s_max, g + 1)
                if after(u, c, 2):
                    act.wait_ge(s_pT_ps, g - 1)
                    act.wait_ge(s_inv, g - 1)
                for j in range(GROUP):
                    last = act.activation(probs[:, c % 2, j, 0:K], b_sc[:, j * K:(j + 1) * K], ACT.Exp,
                                          bias=neg_max[:, c % 2, j:j + 1],
                                          accum_out=probs[:, c % 2, j, K:K + 1])
                last.then_inc(s_prob, 1)

            def score_exp(u, c):
                p = 2 * u + c // 2
                half = PT * ((c // 2) % 2)
                act.wait_ge(s_lmax, p + 1)
                act.activation(rows[:, half:half + PT, EXP_LG], lg_max[:, :], ACT.Exp, scale=-1.0).then_inc(s_elg, 1)

            def first_roots(u, c, lo, hi):
                act.wait_ge(s_xsq if hi == 1 else s_zsq, RING * u + c + 1 if hi == 1 else RING * u + c - 2)
                act.activation(ln_sq[:, lo:hi, :], sq[:, c % 2, lo:hi, :], ACT.Ln).then_inc(s_lnsq, 1)
                act.wait_ge(s_lnsq, RING * u + c + 1)
                act.activation(root0[:, lo:hi, :], ln_sq[:, lo:hi, :], ACT.Exp, scale=-0.5).then_inc(s_root0, 1)

            def z_norm(u, c):
                g, slot, h = RING * u + c, c % RING, (c + 1) % 2
                act.wait_ge(s_zb, g + 1)
                for j in range(GROUP):
                    if after(u, c, RING):
                        act.wait_ge(sent[slot][j], 16 * (u + c // RING))
                    last = act.activation(rows[:, GROUP * slot + j, 0:H], x1[:, c % 2, j, :], ACT.Identity,
                                          bias=root[:, h, 3, j:j + 1], scale=root[:, h, 1, j:j + 1])
                last.then_inc(s_z, 1)
                act.activation(rows[:, GROUP * slot:GROUP * slot + GROUP, Z_ROOT:Z_BIAS + 1],
                               root[:, h, 1:4, :].rearrange("p r j -> p j r"), ACT.Copy).then_inc(s_zroot, 1)

            def step(u, c):
                last_probs = isinstance(u, int) and c == GROUPS + 1
                if last_probs:
                    copy_probs(u, c - 2)
                    copy_values(u, c - 2)
                if live(u, c - 4, GROUPS):
                    copy_z(u, c - 4)
                if live(u, c - 1, GROUPS):
                    copy_n1(u, c - 1)
                    copy_context(u, c - 1)
                lo, hi = (0 if live(u, c, GROUPS) else 1), (3 if live(u, c - 3, GROUPS) else 1)
                if lo < hi:
                    first_roots(u, c, lo, hi)
                if isinstance(u, int) and c == 0:
                    prepare()
                if live(u, c - 2, GROUPS) and not last_probs:
                    copy_probs(u, c - 2)
                    copy_values(u, c - 2)
                if live(u, c - 3, GROUPS):
                    z_norm(u, c - 3)
                if live(u, c - 1, GROUPS):
                    softmax_exp(u, c - 1)
                if chosen(u, c):
                    score_exp(u, c - 5)

            run_steps(act, step, GROUPS + 3, 2 * RING, GROUPS)
            act.preload_act_table_set("silu_and_others")

            act.wait_ge(s_big, 16 * WEIGHTS)
            for e in range(E + 1):
                act.activation(gate_up_hi[:, e], gate_up[:, e], ACT.Copy).then_inc(s_gu_hi, 1)

            act.wait_ge(s_fill_row, 1)
            for e in range(E // 2, E):
                at = act.value_load(fill_row[0:1, e:e + 1], min_val=0, max_val=E * REGION)
                act.dma_start(scratch[bass.ds(at, P), :], filling[:, :]).then_inc(s_fill, 16)
            act.activation(down[:, :, :, :], down_raw[:, :, :, :], ACT.Copy, scale=tanh_g[:, 1:2]).then_inc(s_down, 1)

            def affine2(u, c):
                n, h = RING * u + c, c % 2
                act.wait_ge(s_zT2_ps, n + 1)
                if after(u, c, 2):
                    act.wait_ge(s_gus, n - 1)
                cols = slice(0, P * tiles_of(u, c))
                act.activation(xf_hi[:, h, cols], b_zT2[:, cols], ACT.Identity, bias=lnb[:, :], scale=lnw[:, :])
                act.activation(xfT2[:, h, cols], b_zT2[:, cols], ACT.Identity, bias=lnb[:, :],
                               scale=lnw[:, :]).then_inc(s_xfT2, 1)

            def silus(u, c):
                n, slot = RING * u + c, c % RING
                act.wait_ge(s_score, n + 1)
                for i in range(tiles_of(u, c)):
                    act.wait_ge(s_gur, 2 * n + i + 1)
                    if after(u, c, 1):
                        act.wait_ge(s_hr, 2 * n + i - 1)
                    act.activation(act_r[:, i], b_gur[i][:, 0:I], ACT.Silu,
                                   scale=score[:, slot, i:i + 1]).then_inc(s_ar, 1)
                act.wait_ge(s_gus, n + 1)
                if after(u, c, 1):
                    act.wait_ge(s_hs, n)
                cols = slice(0, P * tiles_of(u, c))
                act.activation(act_s[:, :, cols], gus_v[0][:, :, cols], ACT.Silu).then_inc(s_as, 1)

            def step2(u, c):
                if live(u, c, TILE_PAIRS):
                    affine2(u, c)
                if live(u, c - 1, TILE_PAIRS):
                    silus(u, c - 1)

            run_steps(act, step2, TILE_PAIRS, RING, TILE_PAIRS - RING)

        @block.vector
        def _(dve):
            def x_stats(u, c):
                g, slot = RING * u + c, c % RING
                dve.wait_ge(x_in[slot], 16 * (u + c // RING + 1))
                if after(u, c, 2):
                    dve.wait_ge(s_n1, g - 1)
                for j in range(GROUP):
                    last = dve.bn_stats(x_st[:, j, :], x_sb[:, slot, j, :])
                last.then_inc(s_xst, 1)

            def x_moments(u, c):
                for j in range(GROUP):
                    last = dve.bn_aggr(x_mv[:, c % 2, j, :], x_st[:, j, :])
                last.then_inc(s_xmv, 1)

            def score_max(u, c):
                g = RING * u + c
                dve.wait_ge(s_sc, g + 1)
                if after(u, c, 2):
                    dve.wait_ge(s_prob, g - 1)
                dve.tensor_reduce(neg_max[:, c % 2], b_sc[:, 0:GROUP * K].rearrange("p (j k) -> p j k", k=K),
                                  AX_X, ALU.max, negate=True).then_inc(s_max, 1)

            def row_scale(u, c):
                g = RING * u + c
                dve.wait_ge(s_prob, g + 1)
                dve.reciprocal(row_inv[:, :], probs[:, c % 2, :, K]).then_inc(s_inv, 1)

            def residual(u, c, x_stats_done):
                g, slot = RING * u + c, c % RING
                dve.wait_ge(s_inv, g + 1)
                dve.wait_ge(s_att, g + 1)
                if after(u, c, 2):
                    dve.wait_ge(s_z, g - 1)
                for j in range(GROUP):
                    if j == GROUP - 1 and x_stats_done is not None:
                        dve.wait_ge(s_xst, x_stats_done)
                    last = dve.scalar_tensor_tensor(x1[:, c % 2, j, :], b_att[:, j * H:(j + 1) * H],
                                                    row_inv[:, j:j + 1], x_sb[:, slot, j, :], ALU.mult, ALU.add)
                last.then_inc(s_x1, 1)

            def z_stats(u, c):
                dve.wait_ge(s_x1, RING * u + c + 1)
                for j in range(GROUP):
                    last = dve.bn_stats(z_st[:, j, :], x1[:, c % 2, j, :])
                last.then_inc(s_zst, 1)

            def z_moments(u, c):
                for j in range(GROUP):
                    last = dve.bn_aggr(z_mv[:, c % 2, j, :], z_st[:, j, :])
                last.then_inc(s_zmv, 1)

            def x_square(u, c, z_stats_done):
                dve.wait_ge(s_xmv, RING * u + c + 1)
                if z_stats_done is not None:
                    dve.wait_ge(s_zst, z_stats_done)
                dve.tensor_scalar(sq[:, c % 2, 0, :], x_mv[:, c % 2, :, 1], EPS, float(H),
                                  ALU.add, ALU.mult).then_inc(s_xsq, 1)

            def z_squares(u, c):
                dve.wait_ge(s_zmv, RING * u + c + 1)
                var = z_mv[:, c % 2, :, 1]
                dve.tensor_scalar(sq[:, (c + 1) % 2, 1, :], var, 1.0 + EPS, EPS * EPS, ALU.mult, ALU.add)
                dve.tensor_scalar(sq[:, (c + 1) % 2, 2, :], var, EPS, None, ALU.add).then_inc(s_zsq, 1)

            def root_square(u, c, lo, hi):
                dve.wait_ge(s_root0, RING * u + c + 1)
                dve.tensor_tensor(root0_2[:, lo:hi, :], root0[:, lo:hi, :], root0[:, lo:hi, :], ALU.mult).then_inc(s_root02, 1)

            def root_error(u, c, lo, hi):
                dve.wait_ge(s_root02, RING * u + c + 1)
                dve.scalar_tensor_tensor(root_err[:, lo:hi, :], root0_2[:, lo:hi, :], -0.5, sq[:, c % 2, lo:hi, :],
                                         ALU.mult, ALU.mult).then_inc(s_rerr, 1)

            def root_refined(u, c, lo, hi):
                t = RING * u + c
                dve.wait_ge(s_rerr, t + 1)
                if after(u, c, 5):
                    dve.wait_ge(s_zroot, t - 4)
                dve.scalar_tensor_tensor(root[:, c % 2, lo:hi, :], root_err[:, lo:hi, :], 1.5, root0[:, lo:hi, :],
                                         ALU.add, ALU.mult).then_inc(s_root, 1)

            def x_scalars(u, c):
                g = RING * u + c
                dve.wait_ge(s_root, g + 1)
                dve.scalar_tensor_tensor(x_bias[:, c % 2], x_mv[:, c % 2, :, 0], -1.0, root[:, c % 2, 0, :],
                                         ALU.mult, ALU.mult).then_inc(s_xb, 1)

            def z_scalars(u, c):
                h = (c + 1) % 2
                dve.wait_ge(s_root, RING * u + c + 4)
                dve.scalar_tensor_tensor(root[:, h, 3, :], z_mv[:, c % 2, :, 0], -1.0, root[:, h, 1, :],
                                         ALU.mult, ALU.mult).then_inc(s_zb, 1)

            rev = expert_rev[:, :].rearrange("p (a e) -> p a e", a=1).to_broadcast([P, PT, E])

            def over_experts(v):
                return v.rearrange("p (t a) -> p t a", a=1).to_broadcast([P, PT, E])

            def top_logit(u, c):
                p = 2 * u + c // 2
                dve.wait_ge(s_lg, 2 * p + 2)
                if after(u, c, 2):
                    dve.wait_ge(s_elg, p)
                dve.tensor_reduce(lg_max[:, :], lg_ps, AX_X, ALU.max).then_inc(s_lmax, 1)

            def hits(u, c):
                dve.wait_ge(s_lmax, 2 * u + c // 2 + 1)
                dve.tensor_tensor(hit[:, :, :], lg_ps, over_experts(lg_max[:, :]), ALU.is_equal).then_inc(s_hit, 1)

            def hits_reversed(u, c):
                dve.wait_ge(s_hit, 2 * u + c // 2 + 1)
                dve.tensor_tensor(hit_rev[:, :, :], hit[:, :, :], rev, ALU.mult).then_inc(s_rev, 1)

            def first_hit(u, c):
                dve.wait_ge(s_rev, 2 * u + c // 2 + 1)
                dve.tensor_reduce(best_rev[:, :], hit_rev[:, :, :], AX_X, ALU.max).then_inc(s_best, 1)

            def choose(u, c):
                p = 2 * u + c // 2
                dve.wait_ge(s_best, p + 1)
                if after(u, c, 2):
                    dve.wait_ge(s_rank, p)
                dve.tensor_tensor(onehot[:, 0:PT, :], rev, over_experts(best_rev[:, :]), ALU.is_equal).then_inc(s_hot, 1)

            def places(u, c):
                p = 2 * u + c // 2
                dve.wait_ge(s_rank, p + 1)
                dve.wait_ge(s_free, p + 1)
                free = first_free[:, :].rearrange("p (a e) -> p a e", a=1).to_broadcast([P, PT, E])
                dve.tensor_tensor(place[:, :, :], rank_ps[:, 0:PT, :], free, ALU.add).then_inc(s_place, 1)

            def next_free(u, c):
                p = 2 * u + c // 2
                dve.wait_ge(s_place, p + 1)
                dve.tensor_tensor(first_free[:, :], rank_ps[:, PT, :], first_free[:, :], ALU.add).then_inc(s_free, 1)
                dve.wait_ge(s_hot, p + 1)
                dve.tensor_tensor(place_hit[:, :, :], place[:, :, :], onehot[:, 0:PT, :], ALU.mult).then_inc(s_phit, 1)

            def position(u, c):
                dve.wait_ge(s_phit, 2 * u + c // 2 + 1)
                dve.tensor_reduce(pos_f[:, :], place_hit[:, :, :], AX_X, ALU.add).then_inc(s_posf, 1)

            def row_numbers(u, c):
                dve.wait_ge(s_posf, 2 * u + c // 2 + 1)
                if after(u, c, RING):
                    dve.wait_ge(s_token, RING * u + c + 2)
                dve.tensor_copy(pos[:, (c // 2) % 2, :], pos_f[:, :]).then_inc(s_pos, 1)

            dve.wait_ge(s_const, CONSTS)

            def step(u, c):
                has_x, has_z, has_scores = live(u, c, GROUPS), live(u, c - 3, GROUPS), live(u, c - 1, GROUPS)
                choice = chosen(u, c)
                pair = placed_pair(u, c)
                at_end = isinstance(u, int) and c > GROUPS
                between = choice and not at_end
                place_now = pair is not None and c % 2 == 0
                if has_z:
                    row_scale(u, c - 3)
                if has_x:
                    x_stats(u, c)
                if has_z:
                    residual(u, c - 3, RING * u + c + 1 if has_x else None)
                if has_x:
                    if not has_z:
                        dve.wait_ge(s_xst, c + 1)
                    x_moments(u, c)
                if has_z:
                    z_stats(u, c - 3)
                if has_z and not has_x:
                    dve.wait_ge(s_zst, c - 2)
                if has_x:
                    x_square(u, c, RING * u + c - 2 if has_z else None)
                if has_z:
                    z_moments(u, c - 3)
                if place_now:
                    places(u, pair)
                if has_z:
                    z_squares(u, c - 3)
                if place_now:
                    next_free(u, pair)
                    position(u, pair)
                    row_numbers(u, pair)
                lo, hi = (0 if has_x else 1), (3 if has_z else 1)
                if lo < hi:
                    root_square(u, c, lo, hi)
                    if between:
                        top_logit(u, c - 5)
                    root_error(u, c, lo, hi)
                    if between:
                        hits(u, c - 5)
                    root_refined(u, c, lo, hi)
                    if between:
                        hits_reversed(u, c - 5)
                if has_x:
                    x_scalars(u, c)
                if between:
                    first_hit(u, c - 5)
                if has_z:
                    z_scalars(u, c - 3)
                if has_scores:
                    score_max(u, c - 1)
                if between:
                    choose(u, c - 5)
                if choice and not between:
                    for part in (top_logit, hits, hits_reversed, first_hit, choose):
                        part(u, c - 5)
                if pair is not None and not place_now:
                    for part in (places, next_free, position, row_numbers):
                        part(u, pair)

            run_steps(dve, step, GROUPS + 3, 2 * RING, GROUPS)

            made = [0]

            def link(ins):
                made[0] += 1
                ins.then_inc(s_tab, 1)
                dve.wait_ge(s_tab, made[0])

            NT = TOKENS // P
            dve.wait_ge(s_free, PAIRS + 1)
            dve.tensor_copy(fill_row[:, :], first_free[:, :]).then_inc(s_fill_row, 1)
            link(dve.tensor_tensor(counts[:, :], first_free[:, :], region_at[:, :], ALU.subtract))
            link(dve.tensor_tensor(over[:, :, :], counts[:, :].rearrange("p (e a) -> p e a", a=1).to_broadcast([P, E, NT]),
                                   steps128[:, :].rearrange("p (a n) -> p a n", a=1).to_broadcast([P, E, NT]), ALU.is_gt))
            link(dve.tensor_reduce(n_tiles[:, :], over[:, :, :], AX_X, ALU.add))
            link(dve.tensor_copy(cum[:, 0, :], n_tiles[:, :]))
            for i, d in enumerate((1, 2, 4)):
                link(dve.tensor_copy(cum[:, i + 1, 0:d], cum[:, i, 0:d]))
                link(dve.tensor_tensor(cum[:, i + 1, d:E], cum[:, i, d:E], cum[:, i, 0:E - d], ALU.add))
            cums = cum[:, 3, :].rearrange("p (a e) -> p a e", a=1).to_broadcast([P, TILES, E])
            link(dve.tensor_tensor(past[:, :, :], tile_no[:, :].rearrange("p (t a) -> p t a", a=1).to_broadcast([P, TILES, E]),
                                   cums, ALU.is_ge))
            link(dve.tensor_reduce(tile_e[:, :], past[:, :, :], AX_X, ALU.add))
            link(dve.tensor_tensor(past_cum[:, :, :], past[:, :, :], cums, ALU.mult))
            link(dve.tensor_reduce(tile_c[:, :], past_cum[:, :, :], AX_X, ALU.max))
            link(dve.tensor_tensor(tile_a[:, :], tile_no[:, :], tile_c[:, :], ALU.subtract))
            link(dve.tensor_scalar(tile_b[:, :], tile_e[:, :], float(REGION), None, ALU.mult))
            link(dve.scalar_tensor_tensor(tile_c[:, :], tile_a[:, :], float(P), tile_b[:, :], ALU.mult, ALU.add))
            link(dve.tensor_scalar(tile_row[:, :], tile_c[:, :], float(E * REGION), None, ALU.min))
            link(dve.tensor_scalar(tile_a[:, :], tile_e[:, :], float(E - 1), None, ALU.min))
            link(dve.tensor_tensor(placed[:, :, :], tile_a[:, :].rearrange("p (w i) -> p w i", i=BODY),
                                   bit_place[:, :].rearrange("p (a i) -> p a i", a=1).to_broadcast([P, TILES // BODY, BODY]),
                                   ALU.mult))
            link(dve.tensor_reduce(body_experts_f[:, :], placed[:, :, :], AX_X, ALU.add))
            link(dve.tensor_copy(body_experts[:, :], body_experts_f[:, :]))
            dve.engine_nop().then_inc(s_table, 1)

            for e in range(E + 1):
                dve.wait_ge(s_gu_hi, e + 1)
                dve.tensor_tensor(gate_up_lo[:, e], gate_up[:, e], gate_up_hi[:, e].bitcast(F32),
                                  ALU.subtract).then_inc(s_gu_lo, 1)

            def scalars(u, c):
                n, slot = RING * u + c, c % RING
                tiles = tiles_of(u, c)
                col = [srow[:, slot, 0:tiles, at] for at in range(ROW)]
                dve.wait_ge(r_in[slot], 32 * (u + c // RING) + 16 * tiles)
                if after(u, c, 1):
                    dve.wait_ge(s_scalars, n)
                dve.tensor_scalar(exp_lg1[:, 0:tiles], col[EXP_LG], 1.0, None, ALU.add)
                dve.reciprocal(z_len[:, 0:tiles], col[Z_ROOT])
                dve.tensor_scalar(ln_factor[:, 0:tiles], col[LN_ROOT], tanh_g[:, 1:2], 1.0, ALU.mult, ALU.add).then_inc(s_part, 1)
                dve.wait_ge(s_part, n + 1)
                if after(u, c, RING):
                    dve.wait_ge(s_base, n - RING + 1)
                dve.reciprocal(score[:, slot, 0:tiles], exp_lg1[:, 0:tiles]).then_inc(s_score, 1)
                dve.tensor_tensor(z_scale[:, slot, 0:tiles], ln_factor[:, 0:tiles], z_len[:, 0:tiles], ALU.mult)
                dve.scalar_tensor_tensor(mean[:, slot, 0:tiles], col[Z_BIAS], -1.0, z_len[:, 0:tiles], ALU.mult, ALU.mult).then_inc(s_scalars, 1)

            def xf_rest(u, c):
                n, h = RING * u + c, c % 2
                dve.wait_ge(s_xfT2, n + 1)
                if after(u, c, 2):
                    dve.wait_ge(s_gus, n - 1)
                cols = slice(0, P * tiles_of(u, c))
                dve.tensor_tensor(xf_lo[:, h, cols], xfT2[:, h, cols], xf_hi[:, h, cols].bitcast(F32),
                                  ALU.subtract).then_inc(s_xf_lo, 1)

            def hiddenT(u, c):
                n, h = RING * u + c, c % 2
                dve.wait_ge(s_hT_ps, n + 1)
                if after(u, c, 2):
                    dve.wait_ge(s_dn, n - 1)
                tiles = tiles_of(u, c)
                dve.tensor_copy(hidT_r[:, h, 0:tiles], b_hT[:, 0:tiles * I].rearrange("p (i m) -> p i m", i=tiles)).then_inc(s_hT, 1)

            def hidden(u, c):
                n, slot, h = RING * u + c, c % RING, c % 2
                cols = slice(0, P * tiles_of(u, c))
                for i in range(tiles_of(u, c)):
                    dve.wait_ge(s_ar, 2 * n + i + 1)
                    if after(u, c, 1):
                        dve.wait_ge(s_hT_ps, n)
                    dve.scalar_tensor_tensor(hid_r[:, i], b_gur[i][:, I:2 * I], score[:, slot, i:i + 1],
                                             act_r[:, i], ALU.mult, ALU.mult).then_inc(s_hr, 1)
                dve.wait_ge(s_as, n + 1)
                if after(u, c, 2):
                    dve.wait_ge(s_dn, n - 1)
                dve.tensor_tensor(hid_s[:, h, :, cols], gus_v[1][:, :, cols], act_s[:, :, cols], ALU.mult).then_inc(s_hs, 1)

            def result(u, c):
                n, slot = RING * u + c, c % RING
                dve.wait_ge(s_dn, n + 1)
                dve.wait_ge(s_base, n + 1)
                if after(u, c, RING):
                    dve.wait_ge(stored[slot], 32 * (u + c // RING))
                tiles = tiles_of(u, c)
                dve.tensor_tensor(res[:, slot, 0:tiles], b_dn[:, 0:tiles * H].rearrange("p (i h) -> p i h", i=tiles),
                                  base[:, slot, 0:tiles],
                                  ALU.add).then_inc(s_res, 1)

            def step2(u, c):
                if live(u, c - 2, TILE_PAIRS):
                    hiddenT(u, c - 2)
                if live(u, c, TILE_PAIRS):
                    scalars(u, c)
                    xf_rest(u, c)
                if live(u, c - 1, TILE_PAIRS):
                    hidden(u, c - 1)
                if live(u, c - 2, TILE_PAIRS):
                    result(u, c - 2)

            run_steps(dve, step2, TILE_PAIRS + 1, RING, TILE_PAIRS - RING)

        @block.tensor
        def _(pe):
            pe.wait_ge(s_const, CONSTS)
            pe.wait_ge(s_small, SMALL)
            pe.transpose(b_sc[:, 0:H], w_out_sb[:, :], ident[:, :]).then_inc(s_woT, 1)
            pe.wait_ge(s_wo, 3)

            def transposes(u, c):
                g, slot = RING * u + c, c % RING
                pe.wait_ge(s_n1, g + 1)
                if after(u, c, 1):
                    pe.wait_ge(s_n1T, g)
                for j in range(GROUP):
                    last = pe.transpose(b_n1T[:, j * P:(j + 1) * P], n1[:, c % 2, j, :], ident[:, :])
                last.then_inc(s_n1T_ps, 1)
                pe.wait_ge(c_in[slot], 16 * (u + c // RING + 1))
                if after(u, c, 1):
                    pe.wait_ge(s_ctxT, g)
                for j in range(GROUP):
                    last = pe.transpose(b_ctxT[:, j * K:(j + 1) * K], ctx_sb[0:K, slot, j, :], ident[0:K, 0:K])
                last.then_inc(s_ctxT_ps, 1)

            def z_transposes(u, c):
                g, slot = RING * u + c, c % RING
                pe.wait_ge(s_z, g + 1)
                if after(u, c, 1):
                    pe.wait_ge(s_zT, g)
                for j in range(GROUP):
                    last = pe.transpose(b_zT[:, j * P:(j + 1) * P], rows[:, GROUP * slot + j, 0:H], ident[:, :])
                last.then_inc(s_zT_ps, 1)

            def scores(u, c):
                g = RING * u + c
                pe.wait_ge(s_n1T, g + 1)
                pe.wait_ge(s_ctxT, g + 1)
                if after(u, c, 1):
                    pe.wait_ge(s_prob, g)
                for j in range(GROUP):
                    last = pe.matmul(b_sc[:, j * K:(j + 1) * K], n1T[:, j * P:(j + 1) * P],
                                     ctxT[:, j * K:(j + 1) * K], start=True, stop=True)
                last.then_inc(s_sc, 1)

            def values(u, c):
                g = RING * u + c
                pe.wait_ge(s_ctxT, g + 1)
                if after(u, c, 1):
                    pe.wait_ge(s_val, g)
                for j in range(GROUP):
                    last = pe.matmul(b_val[0:K, j * H:(j + 1) * H], ctxT[:, j * K:(j + 1) * K], w_out_t[:, :],
                                     start=True, stop=True)
                last.then_inc(s_val_ps, 1)

            def logits(u, c):
                g = RING * u + c
                p = 2 * u + c // 2
                pe.wait_ge(s_zT, g + 1)
                pe.wait_ge(s_router, 3)
                if after(u, c, 2) and c % 2 == 0:
                    pe.wait_ge(s_free, p + 1)
                first = (c % 2) * GROUP
                pe.matmul(lg_ps[:, first:first + GROUP, :], lnb_b[:, :], router_x4[:, :, :], start=True, stop=False)
                for j in range(GROUP):
                    last = pe.matmul(lg_ps[:, first + j, :], zT[:, j * P:(j + 1) * P], router_w_ln[:, :],
                                     start=False, stop=(j == GROUP - 1))
                last.then_inc(s_lg, 1)

            def probs_transposes(u, c):
                g = RING * u + c
                pe.wait_ge(s_prob, g + 1)
                if after(u, c, 1):
                    pe.wait_ge(s_pT, g)
                for j in range(GROUP):
                    last = pe.transpose(b_pT[0:K + 1, j * P:(j + 1) * P], probs[:, c % 2, j, :], ident[:, :])
                last.then_inc(s_pT_ps, 1)

            def attend(u, c):
                g = RING * u + c
                pe.wait_ge(s_pT, g + 1)
                pe.wait_ge(s_val, g + 1)
                if after(u, c, 1):
                    pe.wait_ge(s_x1, g)
                for j in range(GROUP):
                    last = pe.matmul(b_att[:, j * H:(j + 1) * H], probsT[0:K + 1, j * P:(j + 1) * P],
                                     vals[0:K + 1, c % 2, j * H:(j + 1) * H], start=True, stop=True)
                last.then_inc(s_att, 1)

            def ranks(u, c):
                p = 2 * u + c // 2
                pe.wait_ge(s_hot, p + 1)
                pe.wait_ge(s_free, p + 1)
                pe.matmul(rank_ps, before[:, :], onehot[:, :, :], start=True, stop=False)
                for t in range(PT):
                    later = PT - t
                    last = pe.matmul(rank_ps[:, t + 1:PT + 1, :], ones[:, :],
                                     onehot[:, t:t + 1, :].to_broadcast([P, later, E]),
                                     start=False, stop=(t == PT - 1))
                last.then_inc(s_rank, 1)

            def step(u, c):
                last_probs = isinstance(u, int) and c == GROUPS + 1
                if last_probs:
                    probs_transposes(u, c - 2)
                if live(u, c - 4, GROUPS):
                    z_transposes(u, c - 4)
                if live(u, c - 1, GROUPS):
                    transposes(u, c - 1)
                if c % 2 == 0 and live(u, c - 6, GROUPS):
                    ranks(u, c - 6)
                if last_probs:
                    attend(u, c - 2)
                if live(u, c - 2, GROUPS) and not last_probs:
                    probs_transposes(u, c - 2)
                if c % 2 == 1 and live(u, c - 4, GROUPS):
                    logits(u, c - 4)
                if live(u, c - 1, GROUPS):
                    scores(u, c - 1)
                if c % 2 == 0 and live(u, c - 4, GROUPS):
                    logits(u, c - 4)
                if live(u, c - 2, GROUPS) and not last_probs:
                    attend(u, c - 2)
                if live(u, c - 1, GROUPS):
                    values(u, c - 1)
                if isinstance(u, int) and c == GROUPS + 3:
                    ranks(u, c - 5)

            run_steps(pe, step, GROUPS + 3, 2 * RING, GROUPS)

            pe.wait_ge(s_table, 1)

            def z_transpose(u, c):
                n, slot = RING * u + c, c % RING
                pe.wait_ge(r_in[slot], 32 * (u + c // RING) + 16 * tiles_of(u, c))
                if after(u, c, 1):
                    pe.wait_ge(s_xfT2, n)
                for i in range(tiles_of(u, c)):
                    last = pe.transpose(b_zT2[:, i * P:(i + 1) * P], srow[:, slot, i, 0:H], ident[:, :])
                last.then_inc(s_zT2_ps, 1)

            def experts_of_body(u):
                word = pe.value_load(body_experts[0:1, bass.ds(u, 1)], min_val=0, max_val=8 ** BODY - 1)
                return [[(word >> 3 * (2 * c + i)) & 7 for i in range(2)] for c in range(RING)]

            def gate_and_up(u, c, experts):
                n, h = RING * u + c, c % 2
                if isinstance(u, int) and c == 0:
                    pe.wait_ge(s_gu_lo, E + 1)
                    pe.wait_ge(s_down, 1)
                pe.wait_ge(s_xf_lo, n + 1)
                cols = slice(0, P * tiles_of(u, c))
                for i in range(tiles_of(u, c)):
                    tile = slice(i * P, (i + 1) * P)
                    if after(u, c, 1):
                        pe.wait_ge(s_hr, 2 * n + i - 1)
                    for k, (xf, w) in enumerate(((xf_hi, gate_up_lo), (xf_lo, gate_up_hi), (xf_hi, gate_up_hi))):
                        last = pe.matmul(b_gur[i][:, :], xf[:, h, tile],
                                         w[:, bass.ds(experts[i], 1), :].rearrange("p a n -> p (a n)"),
                                         start=(k == 0), stop=(k == 2))
                    last.then_inc(s_gur, 1)
                if after(u, c, 1):
                    pe.wait_ge(s_hs, n)
                for bank in range(2):
                    for m in range(CHUNKS):
                        at = slice(bank * I + m * P, bank * I + (m + 1) * P)
                        for k, (xf, w) in enumerate(((xf_hi, gate_up_lo), (xf_lo, gate_up_hi), (xf_hi, gate_up_hi))):
                            last = pe.matmul(gus_v[bank][:, m, cols], w[:, E, at], xf[:, h, cols],
                                             start=(k == 0), stop=(k == 2))
                last.then_inc(s_gus, 1)

            def hidden_transposes(u, c):
                n = RING * u + c
                pe.wait_ge(s_hr, 2 * n + tiles_of(u, c))
                if after(u, c, 1):
                    pe.wait_ge(s_hT, n)
                for i in range(tiles_of(u, c)):
                    for m in range(CHUNKS):
                        at = i * I + m * P
                        last = pe.transpose(b_hT[:, at:at + P], hid_r[:, i, m * P:(m + 1) * P], ident[:, :])
                last.then_inc(s_hT_ps, 1)

            def down_products(u, c, experts):
                n, h = RING * u + c, c % 2
                pe.wait_ge(s_hs, n + 1)
                pe.wait_ge(s_hT, n + 1)
                if after(u, c, 1):
                    pe.wait_ge(s_res, n)
                for i in range(tiles_of(u, c)):
                    acc = b_dn[:, i * H:(i + 1) * H]
                    for m in range(CHUNKS):
                        pe.matmul(acc, hid_s[:, h, m, i * P:(i + 1) * P], down[:, E, m, :], start=(m == 0), stop=False)
                    for m in range(CHUNKS):
                        last = pe.matmul(acc, hidT_r[:, h, i, m * P:(m + 1) * P],
                                         down[:, bass.ds(experts[i], 1), m, :].rearrange("p a n -> p (a n)"),
                                         start=False, stop=(m == CHUNKS - 1))
                last.then_inc(s_dn, 1)

            def step2(u, c, experts):
                if live(u, c, TILE_PAIRS):
                    z_transpose(u, c)
                if live(u, c - 1, TILE_PAIRS):
                    gate_and_up(u, c - 1, experts[c - 1])
                if live(u, c - 2, TILE_PAIRS):
                    down_products(u, c - 2, experts[c - 2])
                if live(u, c - 1, TILE_PAIRS):
                    hidden_transposes(u, c - 1)

            first = experts_of_body(0)
            for c in range(RING):
                step2(0, c, first)
            with pe.Fori(1, TILE_PAIRS // RING - 1) as u:
                experts = experts_of_body(u) + experts_of_body(u - 1)
                for c in range(RING):
                    step2(u, c, experts)
            last_body = TILE_PAIRS // RING - 1
            last = experts_of_body(last_body - 1) + experts_of_body(last_body)
            for c in range(TILE_PAIRS - RING, TILE_PAIRS + 2):
                step2(0, c, {RING * (last_body - 1) + i: e for i, e in enumerate(last)})


_INS = ["x", "ctx_1024", "g_xattn", "g_ffn", "L0_xattn_W_out", "L0_xattn_b_out", "L0_ffn_ln_w", "L0_ffn_ln_b",
        "L0_ffn_router_w", "L0_ffn_gate_w", "L0_ffn_up_w", "L0_ffn_down_w", "L0_ffn_sh_gate", "L0_ffn_sh_up",
        "L0_ffn_sh_down"]


def kernel(**inputs):
    import numpy as np
    import concourse.bacc as bacc
    from concourse import mybir as mb
    from concourse.bass_utils import run_bass_kernel_spmd

    nc = bacc.Bacc("TRN2", target_bir_lowering=False, num_devices=1)
    arrays, args = {}, []
    for name in _INS:
        a = np.ascontiguousarray(inputs[name])
        arrays[f"in_{name}"] = a
        args.append(nc.dram_tensor(f"in_{name}", a.shape, mb.dt.from_np(a.dtype), kind="ExternalInput").ap())
    shape = tuple(inputs["x"].shape)
    args.append(nc.dram_tensor("out_0", shape, mb.dt.float32, kind="ExternalOutput").ap())
    flamingo_kernel(nc, *args)
    r = run_bass_kernel_spmd(nc, [arrays], core_ids=[0])
    return r.results[0]["out_0"]
```
